# Optimizing a Trainium2 kernel written in Bass

```python
import numpy as np
import jax
import jax.numpy as jnp

def _softmax(x, axis=-1):
    return jax.nn.softmax(x, axis=axis)

def _gelu(x):
    return jax.nn.gelu(x, approximate=True)

def _silu(x):
    return jax.nn.silu(x)

def _sigmoid(x):
    return jax.nn.sigmoid(x)

def _layernorm(x, axis=-1, eps=1e-05):
    m = jnp.mean(x, axis=axis, keepdims=True)
    v = jnp.var(x, axis=axis, keepdims=True)
    return (x - m) / jnp.sqrt(v + eps)

def _scatter_add(tgt, idx, src, axis=0):
    return tgt.at[idx].add(src)

def _segment_sum(src, seg, n):
    return jax.ops.segment_sum(src, seg, n)
kernel_name = 'mk_dlrm_tower_d1_rec_r8_4a1598'

def setup_inputs(seed: int=0):
    np.random.seed(seed)
    _w = jnp.asarray

    def _rec_inputs():
        import jax
        import jax.numpy as jnp
        _tk = jax.random.key(seed)
        ids = jnp.stack([jax.random.randint(jax.random.fold_in(_tk, 200 + f), (512,), 0, v, jnp.int32) for f, v in enumerate([1250, 125000, 125000, 125000, 1250, 12500, 1250, 1000, 12500, 12500, 1000, 1000, 1000, 12500, 1000, 12500, 12500, 1250, 1250, 1250, 1000, 12500, 1000, 1250, 1000, 1000])], axis=1)
        tbl_0 = 0.05 * jax.random.normal(jax.random.fold_in(_tk, 500 + 0), (1250, 64), jnp.float32)
        tbl_1 = 0.05 * jax.random.normal(jax.random.fold_in(_tk, 500 + 1), (125000, 64), jnp.float32)
        tbl_2 = 0.05 * jax.random.normal(jax.random.fold_in(_tk, 500 + 2), (125000, 64), jnp.float32)
        tbl_3 = 0.05 * jax.random.normal(jax.random.fold_in(_tk, 500 + 3), (125000, 64), jnp.float32)
        tbl_4 = 0.05 * jax.random.normal(jax.random.fold_in(_tk, 500 + 4), (1250, 64), jnp.float32)
        tbl_5 = 0.05 * jax.random.normal(jax.random.fold_in(_tk, 500 + 5), (12500, 64), jnp.float32)
        tbl_6 = 0.05 * jax.random.normal(jax.random.fold_in(_tk, 500 + 6), (1250, 64), jnp.float32)
        tbl_7 = 0.05 * jax.random.normal(jax.random.fold_in(_tk, 500 + 7), (1000, 64), jnp.float32)
        tbl_8 = 0.05 * jax.random.normal(jax.random.fold_in(_tk, 500 + 8), (12500, 64), jnp.float32)
        tbl_9 = 0.05 * jax.random.normal(jax.random.fold_in(_tk, 500 + 9), (12500, 64), jnp.float32)
        tbl_10 = 0.05 * jax.random.normal(jax.random.fold_in(_tk, 500 + 10), (1000, 64), jnp.float32)
        tbl_11 = 0.05 * jax.random.normal(jax.random.fold_in(_tk, 500 + 11), (1000, 64), jnp.float32)
        tbl_12 = 0.05 * jax.random.normal(jax.random.fold_in(_tk, 500 + 12), (1000, 64), jnp.float32)
        tbl_13 = 0.05 * jax.random.normal(jax.random.fold_in(_tk, 500 + 13), (12500, 64), jnp.float32)
        tbl_14 = 0.05 * jax.random.normal(jax.random.fold_in(_tk, 500 + 14), (1000, 64), jnp.float32)
        tbl_15 = 0.05 * jax.random.normal(jax.random.fold_in(_tk, 500 + 15), (12500, 64), jnp.float32)
        tbl_16 = 0.05 * jax.random.normal(jax.random.fold_in(_tk, 500 + 16), (12500, 64), jnp.float32)
        tbl_17 = 0.05 * jax.random.normal(jax.random.fold_in(_tk, 500 + 17), (1250, 64), jnp.float32)
        tbl_18 = 0.05 * jax.random.normal(jax.random.fold_in(_tk, 500 + 18), (1250, 64), jnp.float32)
        tbl_19 = 0.05 * jax.random.normal(jax.random.fold_in(_tk, 500 + 19), (1250, 64), jnp.float32)
        tbl_20 = 0.05 * jax.random.normal(jax.random.fold_in(_tk, 500 + 20), (1000, 64), jnp.float32)
        tbl_21 = 0.05 * jax.random.normal(jax.random.fold_in(_tk, 500 + 21), (12500, 64), jnp.float32)
        tbl_22 = 0.05 * jax.random.normal(jax.random.fold_in(_tk, 500 + 22), (1000, 64), jnp.float32)
        tbl_23 = 0.05 * jax.random.normal(jax.random.fold_in(_tk, 500 + 23), (1250, 64), jnp.float32)
        tbl_24 = 0.05 * jax.random.normal(jax.random.fold_in(_tk, 500 + 24), (1000, 64), jnp.float32)
        tbl_25 = 0.05 * jax.random.normal(jax.random.fold_in(_tk, 500 + 25), (1000, 64), jnp.float32)
        _rk = jax.random.fold_in(_tk, 7)
        r_dense_t = 7.22013e-05 + 1.00017 * jax.random.normal(jax.random.fold_in(_rk, 101), (512, 256), jnp.float32)
        W_top1 = 0.0360844 * jax.random.normal(jax.random.fold_in(_tk, 801), (768, 512), jnp.float32)
        W_top2 = 0.0441942 * jax.random.normal(jax.random.fold_in(_tk, 802), (512, 256), jnp.float32)
        W_top3 = 0.0625 * jax.random.normal(jax.random.fold_in(_tk, 803), (256, 1), jnp.float32)
        b_top1 = jnp.zeros((512,), jnp.float32)
        b_top2 = jnp.zeros((256,), jnp.float32)
        return (r_dense_t, ids, tbl_0, tbl_1, tbl_2, tbl_3, tbl_4, tbl_5, tbl_6, tbl_7, tbl_8, tbl_9, tbl_10, tbl_11, tbl_12, tbl_13, tbl_14, tbl_15, tbl_16, tbl_17, tbl_18, tbl_19, tbl_20, tbl_21, tbl_22, tbl_23, tbl_24, tbl_25, W_top1, b_top1, W_top2, b_top2, W_top3)
    r_dense_t, ids, tbl_0, tbl_1, tbl_2, tbl_3, tbl_4, tbl_5, tbl_6, tbl_7, tbl_8, tbl_9, tbl_10, tbl_11, tbl_12, tbl_13, tbl_14, tbl_15, tbl_16, tbl_17, tbl_18, tbl_19, tbl_20, tbl_21, tbl_22, tbl_23, tbl_24, tbl_25, W_top1, b_top1, W_top2, b_top2, W_top3 = _rec_inputs()

    def _L0_rec_setup():
        import jax, jax.numpy as jnp
        import numpy as np
        EPS = 1e-05
        NI = 33
        TRIL_I, TRIL_J = np.tril_indices(NI, k=-1)

        def layer_norm(x, g, b):
            m = jnp.mean(x, axis=-1, keepdims=True)
            v = jnp.mean(jnp.square(x - m), axis=-1, keepdims=True)
            return (x - m) * jax.lax.rsqrt(v + EPS) * g + b
        key = jax.random.key(seed)
        ks = jax.random.split(key, 8)
        B, D_DENSE, N_SP, D_SP = (4096, 256, 26, 64)
        E, PROJ, MAXD, NFLAT = (128, 32, 512, 528)
        dense_t = jax.random.normal(ks[0], (B, D_DENSE), dtype=jnp.float32)
        sparse_t = jax.random.normal(ks[1], (B, N_SP, D_SP), dtype=jnp.float32)
        Wd = jax.random.normal(ks[2], (E, D_DENSE), dtype=jnp.float32) / np.sqrt(D_DENSE)
        Ws = jax.random.normal(ks[3], (E, D_SP), dtype=jnp.float32) / np.sqrt(D_SP)
        Wsi = jax.random.normal(ks[4], (PROJ, N_SP), dtype=jnp.float32) / np.sqrt(N_SP)
        Wl = jax.random.normal(ks[5], (MAXD, NFLAT), dtype=jnp.float32) / np.sqrt(NFLAT)
        gd = jnp.ones((E,), jnp.float32)
        bd = jnp.zeros((E,), jnp.float32)
        gs = jnp.ones((E,), jnp.float32)
        bs = jnp.zeros((E,), jnp.float32)
        gsi = jnp.ones((PROJ,), jnp.float32)
        bsi = jnp.zeros((PROJ,), jnp.float32)
        gl = jnp.ones((MAXD,), jnp.float32)
        bl = jnp.zeros((MAXD,), jnp.float32)
        return {'dense_t': dense_t, 'sparse_t': sparse_t, 'Wd': Wd, 'gd': gd, 'bd': bd, 'Ws': Ws, 'gs': gs, 'bs': bs, 'Wsi': Wsi, 'gsi': gsi, 'bsi': bsi, 'Wl': Wl, 'gl': gl, 'bl': bl, 'dims_in_use': 384}
    _L0_rec_all = _L0_rec_setup()
    _L0_rec_in = {k: v for k, v in _L0_rec_all.items() if k in ('Wd', 'gd', 'bd', 'Ws', 'gs', 'bs', 'Wsi', 'gsi', 'bsi', 'Wl', 'gl', 'bl')}
    del _L0_rec_all
    return {'r_dense_t': r_dense_t, 'ids': ids, 'tbl_0': tbl_0, 'tbl_1': tbl_1, 'tbl_2': tbl_2, 'tbl_3': tbl_3, 'tbl_4': tbl_4, 'tbl_5': tbl_5, 'tbl_6': tbl_6, 'tbl_7': tbl_7, 'tbl_8': tbl_8, 'tbl_9': tbl_9, 'tbl_10': tbl_10, 'tbl_11': tbl_11, 'tbl_12': tbl_12, 'tbl_13': tbl_13, 'tbl_14': tbl_14, 'tbl_15': tbl_15, 'tbl_16': tbl_16, 'tbl_17': tbl_17, 'tbl_18': tbl_18, 'tbl_19': tbl_19, 'tbl_20': tbl_20, 'tbl_21': tbl_21, 'tbl_22': tbl_22, 'tbl_23': tbl_23, 'tbl_24': tbl_24, 'tbl_25': tbl_25, 'W_top1': W_top1, 'b_top1': b_top1, 'W_top2': W_top2, 'b_top2': b_top2, 'W_top3': W_top3, 'L0_rec_Wd': _L0_rec_in['Wd'], 'L0_rec_gd': _L0_rec_in['gd'], 'L0_rec_bd': _L0_rec_in['bd'], 'L0_rec_Ws': _L0_rec_in['Ws'], 'L0_rec_gs': _L0_rec_in['gs'], 'L0_rec_bs': _L0_rec_in['bs'], 'L0_rec_Wsi': _L0_rec_in['Wsi'], 'L0_rec_gsi': _L0_rec_in['gsi'], 'L0_rec_bsi': _L0_rec_in['bsi'], 'L0_rec_Wl': _L0_rec_in['Wl'], 'L0_rec_gl': _L0_rec_in['gl'], 'L0_rec_bl': _L0_rec_in['bl']}

def reference(r_dense_t, ids, tbl_0, tbl_1, tbl_2, tbl_3, tbl_4, tbl_5, tbl_6, tbl_7, tbl_8, tbl_9, tbl_10, tbl_11, tbl_12, tbl_13, tbl_14, tbl_15, tbl_16, tbl_17, tbl_18, tbl_19, tbl_20, tbl_21, tbl_22, tbl_23, tbl_24, tbl_25, W_top1, b_top1, W_top2, b_top2, W_top3, L0_rec_Wd, L0_rec_gd, L0_rec_bd, L0_rec_Ws, L0_rec_gs, L0_rec_bs, L0_rec_Wsi, L0_rec_gsi, L0_rec_bsi, L0_rec_Wl, L0_rec_gl, L0_rec_bl):
    import jax
    import jax.numpy as jnp

    def _L0_rec_ref(dense_t, sparse_t, Wd, gd, bd, Ws, gs, bs, Wsi, gsi, bsi, Wl, gl, bl, dims_in_use):
        import jax, jax.numpy as jnp
        import numpy as np
        EPS = 1e-05
        NI = 33
        TRIL_I, TRIL_J = np.tril_indices(NI, k=-1)

        def layer_norm(x, g, b):
            m = jnp.mean(x, axis=-1, keepdims=True)
            v = jnp.mean(jnp.square(x - m), axis=-1, keepdims=True)
            return (x - m) * jax.lax.rsqrt(v + EPS) * g + b
        x = layer_norm(dense_t @ Wd.T, gd, bd)
        y = layer_norm(jnp.einsum('bnd,ed->bne', sparse_t, Ws), gs, bs)
        y = jnp.einsum('bne,pn->bep', y, Wsi)
        y = layer_norm(y, gsi, bsi)
        y = jnp.swapaxes(y, 1, 2)
        T = jnp.concatenate([x[:, None, :], y], axis=1)
        Z = jnp.einsum('bnd,bmd->bnm', T, T)
        Zflat = Z[:, TRIL_I, TRIL_J]
        out = layer_norm(Zflat @ Wl.T, gl, bl)
        maxd = out.shape[-1]
        mask = (jnp.arange(maxd) < dims_in_use).astype(out.dtype)
        return out * mask
    e = jnp.stack([tbl_0[ids[:, 0]], tbl_1[ids[:, 1]], tbl_2[ids[:, 2]], tbl_3[ids[:, 3]], tbl_4[ids[:, 4]], tbl_5[ids[:, 5]], tbl_6[ids[:, 6]], tbl_7[ids[:, 7]], tbl_8[ids[:, 8]], tbl_9[ids[:, 9]], tbl_10[ids[:, 10]], tbl_11[ids[:, 11]], tbl_12[ids[:, 12]], tbl_13[ids[:, 13]], tbl_14[ids[:, 14]], tbl_15[ids[:, 15]], tbl_16[ids[:, 16]], tbl_17[ids[:, 17]], tbl_18[ids[:, 18]], tbl_19[ids[:, 19]], tbl_20[ids[:, 20]], tbl_21[ids[:, 21]], tbl_22[ids[:, 22]], tbl_23[ids[:, 23]], tbl_24[ids[:, 24]], tbl_25[ids[:, 25]]], axis=1)
    z = _L0_rec_ref(r_dense_t, e, L0_rec_Wd, L0_rec_gd, L0_rec_bd, L0_rec_Ws, L0_rec_gs, L0_rec_bs, L0_rec_Wsi, L0_rec_gsi, L0_rec_bsi, L0_rec_Wl, L0_rec_gl, L0_rec_bl, 384)
    z = z.reshape(z.shape[0], -1)
    h = jnp.concatenate([z, r_dense_t], axis=1)
    h = jnp.maximum(h @ W_top1 + b_top1, 0.0)
    h = jnp.maximum(h @ W_top2 + b_top2, 0.0)
    y = h @ W_top3
    return y

_drawn_inputs = setup_inputs


def setup_inputs(seed=0):
    import zlib

    import numpy as np

    out = dict(_drawn_inputs(seed))
    spreads = {'b_top1': (0.0, 0.1),
     'b_top2': (0.0, 0.1),
     'L0_rec_gd': (1.0, 0.6),
     'L0_rec_bd': (0.0, 0.8),
     'L0_rec_gs': (1.0, 0.6),
     'L0_rec_bs': (0.0, 0.1),
     'L0_rec_gsi': (1.0, 0.2),
     'L0_rec_bsi': (0.0, 0.1),
     'L0_rec_gl': (1.0, 0.2),
     'L0_rec_bl': (0.0, 0.1)}
    factors = {}
    for name, (base, spread) in spreads.items():
        noise = np.random.default_rng([zlib.crc32(name.encode()), seed]).standard_normal(out[name].shape)
        drawn = base * np.exp(spread * noise) if base else spread * noise
        out[name] = jnp.asarray(drawn.astype(out[name].dtype))
    for name, factor in factors.items():
        out[name] = (out[name] * factor).astype(out[name].dtype)
    return out
```

```python
from contextlib import ExitStack

import concourse.bass as bass
from concourse import mybir

F32 = mybir.dt.float32
F32R = mybir.dt.float32r
BF16 = mybir.dt.bfloat16
I32 = mybir.dt.int32
ALU = mybir.AluOpType
ACT = mybir.ActivationFunctionType
AX_X = mybir.AxisListType.X

P = 128
B = 512
N = 26
D = 64
E = 128
PR = 32
DD = 256
MAXD, DIMS = 512, 384
H1, H2 = 512, 256
EPS = 1e-5

BB = P // PR
R = BB * N
GT = 4
GB = BB * GT
KS = 8
TB = GB * KS
TILES = B // TB
G_LAG, S_LAG, Y_LAG, YN_LAG, Z_LAG = 1, 2, 3, 4, 5
SPREAD, OUTPUTS, ZVAR, NORMALISE, LAYER1, LAYER2, LAYER3 = (9, 13), 15, 19, 20, 20, 22, 23
BACK = LAYER3 // KS
QC = 8
YW = PR + 2
NSPLIT = 9

COLS = {}


def _cols():
    at = 0
    for name, width in [("wsi", PR), ("gs", 1), ("gd", 1), ("bd", 1), ("gp", 1), ("bp", 1), ("gq", QC),
                        ("bq", QC), ("gl", 3), ("bl", 3), ("b1", 4), ("b2", 2), ("w3", 2), ("bs", E)]:
        COLS[name] = (at, at + width)
        at += width
    return at


NPAR = _cols()

CC = {}


def _ccols():
    at = 0
    for name, width in [("ident", P), ("centre", P), ("ones", P), ("eps", 1), ("block", BB), ("mp", PR),
                        ("mq", QC * PR), ("split", 6)]:
        CC[name] = (at, at + width)
        at += width
    return at


NCON = _ccols()


def dlrm_program(nc, table, ids, base, par_d, con_d, ws_d, wd_d, dense_d, wl_d, wx_d, w1_d, w2_d, out):
    with ExitStack() as ctx:
        def sb(name, shape, dt=F32):
            return ctx.enter_context(nc.sbuf_tensor(name, shape, dt))

        def sem(name):
            return ctx.enter_context(nc.semaphore(name))

        par = sb("par", [P, NPAR])
        con = sb("con", [P, NCON])
        idx_all = sb("idx_all", [R, B // BB], I32)
        idx_base = sb("idx_base", [R, 1], I32)
        idx = sb("idx", [R, KS, GT], I32)
        pace = sb("pace", [R, 1], I32)
        ws2 = sb("ws2", [P, P])
        wsc = sb("wsc", [P, P])
        wsg = sb("wsg", [P, P])
        wst = sb("wst", [P, P])
        wst_hi = sb("wst_hi", [P, P], F32R)
        wst_lo = sb("wst_lo", [P, P], F32R)
        gram = sb("gram", [P, P])
        wsic = sb("wsic", [P, PR])
        fold = sb("fold", [R, BB, PR])
        wd = sb("wd", [P, 2, E])
        dense = sb("dense", [P, 2, B])
        wl = sb("wl", [P, QC + 1, MAXD])
        w1 = sb("w1", [P, 5, H1])
        w2 = sb("w2", [P, 4, H2])
        bs_row = sb("bs_row", [NSPLIT, E], BF16)
        sw_row = sb("sw_row", [NSPLIT, GB, PR], BF16)
        split_b = sb("split_b", [NSPLIT, 3, E], BF16)
        split_s = sb("split_s", [NSPLIT, 3, PR], BF16)
        split_f = sb("split_f", [NSPLIT, 4, E])
        mean = sb("mean", [P, 16])
        gg = sb("gg", [P, QC])
        sel = sb("sel", [P, QC, PR + 1])
        sel2 = sb("sel2", [P, QC, PR])
        b1f = sb("b1f", [P, 4])
        xt = sb("xt", [P, B])
        xsq = sb("xsq", [P, B])
        emb = sb("emb", [R, KS, GT * D])
        embt = sb("embt", [P, 2, 2 * R])
        prod = sb("prod", [R, GT, D])
        evar = sb("evar", [R, 2, GT])
        estd = sb("estd", [R, 2, GT])
        erstd = sb("erstd", [R, 2, GT])
        embs = sb("embs", [R, 2, GT * D])
        smat = sb("smat", [P, 2, GB * PR], F32R)
        ysq = sb("ysq", [P, GB, PR])
        yvar = sb("yvar", [P, 2, GB])
        ystd = sb("ystd", [P, 2, GB])
        yrstd = sb("yrstd", [P, 2, GB])
        yn = sb("yn", [P, 2, GB, YW])
        zs = sb("zs", [P, B // GB, GT, YW])
        feat = sb("feat", [P, QC + 1, B])
        zsq = sb("zsq", [P, 4, TB])
        zstd = sb("zstd", [P, TB])
        zrstd = sb("zrstd", [P, TB])
        zn = sb("zn", [P, 3, TB])
        h1 = sb("h1", [P, 4, TB])
        h2 = sb("h2", [P, 2, TB])
        y_out = sb("y_out", [1, B])

        def pb(name):
            return ctx.enter_context(nc.psum_tensor(name, [P, 512], F32))

        ps_t, ps_g, ps_s, ps_z, ps_a, ps_b = (pb(f"ps_{n}") for n in "tgszab")
        ps_y = [pb(f"ps_y{n}") for n in range(2)]

        def pv(name, rows=P):
            a, b = COLS[name]
            return par[0:rows, a:b]

        def cv(name, rows=P):
            a, b = CC[name]
            return con[0:rows, a:b]

        ids_in, par_in, con_in, ws_in = sem("ids_in"), sem("par_in"), sem("con_in"), sem("ws_in")
        dense_in, wd_in, wl_in, w1_in, w2_in = sem("dense_in"), sem("wd_in"), sem("wl_in"), sem("w1_in"), sem("w2_in")
        emb_in = [sem(f"emb_in{k}") for k in range(KS)]
        out_done = sem("out_done")
        idx_done = sem("idx_done")
        cleared = sem("cleared")
        set_pe, set_dve, set_act = sem("set_pe"), sem("set_dve"), sem("set_act")
        chain = sem("chain")
        t_done, embt_done, quad_done, evar_done = sem("t_done"), sem("embt_done"), sem("quad_done"), sem("evar_done")
        estd_done, embs_done, s_done = sem("estd_done"), sem("embs_done"), sem("s_done")
        smat_hi, smat_lo = sem("smat_hi"), sem("smat_lo")
        y_done, ysq_done, yvar_done, ystd_done = sem("y_done"), sem("ysq_done"), sem("yvar_done"), sem("ystd_done")
        prod_done, erstd_done, yrstd_done, zrstd_done = sem("prod_done"), sem("erstd_done"), sem("yrstd_done"), sem("zrstd_done")
        yn_done, z_done, zs_done = sem("yn_done"), sem("z_done"), sem("zs_done")
        feat_done, wl_done, zsq_done, zvar_done = sem("feat_done"), sem("wl_done"), sem("zsq_done"), sem("zvar_done")
        zstd_done, zn_done, l1_done, h1_done = sem("zstd_done"), sem("zn_done"), sem("l1_done"), sem("h1_done")
        l2_done, h2_done, l3_done, y_ready = sem("l2_done"), sem("h2_done"), sem("l3_done"), sem("y_ready")

        block = ctx.enter_context(nc.Block())

        def wait(eng, s, value):
            if not isinstance(value, int) or value > 0:
                eng.wait_ge(s, value)

        def has(s):
            return not isinstance(s, int) or 0 <= s < TILES * KS

        def at(s, n):
            return isinstance(s, int) and s == n

        def tile_work(i, k, works):
            for offset, work in works:
                t = i - offset // KS
                if offset % KS == k and (not isinstance(t, int) or 0 <= t < TILES):
                    work(t)

        def run_steps(eng, step):
            for i in range(BACK):
                for k in range(KS):
                    step(i, k)
            with eng.Fori(BACK, TILES) as i:
                for k in range(KS):
                    step(i, k)
            for i in range(TILES, TILES + BACK):
                for k in range(KS):
                    step(i, k)

        @block.sync
        def _(sp):
            sp.dma_start(idx_base[:, :], base).then_inc(ids_in, 16)
            sp.dma_start(idx_all[:, :], ids).then_inc(ids_in, 16)
            sp.dma_start(con[:, :], con_d).then_inc(con_in, 16)
            sp.dma_start(par[:, :], par_d).then_inc(par_in, 16)
            sp.dma_start(ws2[:, :], ws_d).then_inc(ws_in, 16)
            sp.dma_start(wd[:, :, :], wd_d).then_inc(wd_in, 16)
            sp.dma_start(dense[:, :, :], dense_d).then_inc(dense_in, 16)
            sp.dma_start(wl[:, 0:QC, :], wl_d).then_inc(wl_in, 16)
            sp.wait_ge(cleared, 1)
            sp.dma_start(wl[0:PR, QC, :], wx_d).then_inc(wl_in, 16)
            sp.dma_start(w1[:, :, :], w1_d).then_inc(w1_in, 16)
            sp.dma_start(w2[:, :, :], w2_d).then_inc(w2_in, 16)
            sp.wait_ge(y_ready, TILES)
            sp.dma_start(out, y_out[0:1, :]).then_inc(out_done, 16)
            sp.wait_ge(out_done, 16)

        @block.gpsimd
        def _(pool):
            nc.gpsimd.memset(wl[:, QC, :], 0.0).then_inc(cleared, 1)
            pool.wait_ge(ids_in, 32)

            def gather_tile(i):
                for k in range(KS):
                    if k % 4 == 0:
                        wait(pool, embs_done, KS * i - KS + k + 4)
                        nc.gpsimd.tensor_tensor(idx[:, k:k + 4, :].rearrange("p k t -> p (k t)"),
                                                idx_all[:, bass.ds(KS * GT * i + k * GT, 4 * GT)],
                                                idx_base[:, 0:1].to_broadcast([R, 4 * GT]), ALU.add).then_inc(idx_done, 1)
                        pool.wait_ge(idx_done, 2 * i + k // 4 + 1)
                        nc.gpsimd.tensor_tensor(pace[:, :], idx_base[:, :], idx_base[:, :], ALU.add)
                    for t in range(GT):
                        nc.gpsimd.indirect_dma_start(
                            emb[:, k, t * D:(t + 1) * D], None, table,
                            bass.IndirectOffsetOnAxis(ap=idx[:, k, t:t + 1], axis=0)
                        ).then_inc(emb_in[k], 16)

            gather_tile(0)
            with pool.Fori(1, TILES) as i:
                gather_tile(i)

        @block.tensor
        def _(pe):
            mm = nc.tensor.matmul
            pe.wait_ge(con_in, 16)
            pe.wait_ge(ws_in, 16)
            mm(ps_t[:, 0:P], cv("centre"), ws2[:, :], start=True, stop=True).then_inc(set_pe, 1)
            pe.wait_ge(set_dve, 1)
            mm(ps_g[:, 0:P], wsc[:, :], wsc[:, :], start=True, stop=True).then_inc(set_pe, 1)
            pe.wait_ge(set_dve, 2)
            nc.tensor.transpose(ps_s[:, 0:P], wsg[:, :], cv("ident")).then_inc(set_pe, 1)
            pe.wait_ge(set_dve, 3)
            mm(ps_z[0:NSPLIT, 0:PR], con[0:N, CC["ones"][0]:CC["ones"][0] + NSPLIT], wsic[0:N, :],
               start=True, stop=True).then_inc(set_pe, 1)
            pe.wait_ge(set_dve, 4)
            pe.wait_ge(dense_in, 16)
            for c in range(2):
                last = mm(ps_y[0][:, :], wd[:, c, :], dense[:, c, :], start=c == 0, stop=c == 1)
            last.then_inc(set_pe, 1)
            pe.wait_ge(set_act, 1)
            mm(ps_a[:, :], cv("ones"), xsq[:, :], start=True, stop=True).then_inc(set_pe, 1)
            pe.wait_ge(set_dve, 5)
            mm(ps_b[0:1, :], con[:, CC["ones"][0]:CC["ones"][0] + 1], xt[:, :], start=True, stop=True).then_inc(set_pe, 1)
            pe.wait_ge(set_dve, 6)

            def weights():
                pe.wait_ge(set_dve, 7)
                for c in range(QC):
                    last = mm(ps_a[0:PR + 1, :], sel[:, c, :], wl[:, c, :], start=c == 0, stop=c == QC - 1)
                last.then_inc(set_pe, 1)
                mm(ps_b[0:1, :], par[0:PR, COLS["bp"][0]:COLS["bp"][1]], wl[0:PR, QC, :], start=True, stop=True).then_inc(set_pe, 1)

            def bias1():
                pe.wait_ge(set_dve, 8)
                pe.wait_ge(w1_in, 16)
                for o in range(4):
                    for c in range(3):
                        last = mm(ps_a[:, o:o + 1], w1[:, c, o * P:(o + 1) * P],
                                  par[:, COLS["bl"][0] + c:COLS["bl"][0] + c + 1], start=c == 0, stop=c == 2)
                last.then_inc(set_pe, 1)

            def outputs(t, o):
                if o == 0:
                    pe.wait_ge(feat_done, 2 * t + 2)
                    pe.wait_ge(set_dve, 8)
                    wait(pe, zn_done, t)
                for c in range(QC + 1):
                    last = mm(ps_a[:, o * TB:(o + 1) * TB], wl[:, c, o * P:(o + 1) * P],
                              feat[:, c, bass.ds(TB * t, TB)], start=c == 0, stop=c == QC)
                if o == 3:
                    last.then_inc(wl_done, 1)

            def zvar(t):
                pe.wait_ge(zsq_done, t + 1)
                wait(pe, y_ready, t)
                for o in range(4):
                    last = mm(ps_b[:, 0:TB], cv("ones"), zsq[:, o, :], start=o == 0, stop=o == 3)
                last.then_inc(zvar_done, 1)

            def layer1(t, outs):
                pe.wait_ge(zn_done, t + 1)
                pe.wait_ge(set_dve, 9)
                for o in outs:
                    for c in range(5):
                        rhs = zn[:, c, :] if c < 3 else dense[:, c - 3, bass.ds(TB * t, TB)]
                        last = mm(ps_b[:, o * TB:(o + 1) * TB], w1[:, c, o * P:(o + 1) * P], rhs, start=c == 0, stop=c == 4)
                    if o == 3:
                        last.then_inc(l1_done, 1)

            def layer2(t):
                pe.wait_ge(h1_done, t + 1)
                pe.wait_ge(w2_in, 16)
                for o in range(2):
                    for c in range(4):
                        last = mm(ps_b[:, o * TB:(o + 1) * TB], w2[:, c, o * P:(o + 1) * P], h1[:, c, :],
                                  start=c == 0, stop=c == 3)
                last.then_inc(l2_done, 1)

            def layer3(t):
                pe.wait_ge(h2_done, t + 1)
                for c in range(2):
                    last = mm(ps_b[0:1, 2 * TB:3 * TB], par[:, COLS["w3"][0] + c:COLS["w3"][0] + c + 1], h2[:, c, :],
                              start=c == 0, stop=c == 1)
                last.then_inc(l3_done, 1)

            def step(i, k):
                s = KS * i + k
                if has(s):
                    pe.wait_ge(emb_in[k], 16 * GT * i + 16 * GT)
                    wait(pe, embt_done, s)
                    for h in range(2):
                        last = nc.tensor.transpose(ps_t[:, h * R:(h + 1) * R], emb[:, k, h * P:(h + 1) * P],
                                                   con[0:R, CC["ident"][0]:CC["ident"][0] + R])
                    last.then_inc(t_done, 1)
                g, slot = s - G_LAG, (k - G_LAG) % 2
                if has(g):
                    pe.wait_ge(embt_done, g + 1)
                    wait(pe, prod_done, g)
                    for h in range(2):
                        last = mm(ps_g[0:R, h * P:(h + 1) * P], embt[:, slot, h * R:(h + 1) * R], gram[:, :],
                                  start=True, stop=True)
                    last.then_inc(quad_done, 1)
                g, slot = s - S_LAG, (k - S_LAG) % 2
                if has(g):
                    pe.wait_ge(embs_done, g + 1)
                    wait(pe, smat_lo, g)
                    for h in range(2):
                        last = mm(ps_s[:, h * P:(h + 1) * P], embs[:, slot, h * P:(h + 1) * P],
                                  fold[:, :, :], start=True, stop=True)
                    last.then_inc(s_done, 1)
                g, slot = s - Y_LAG, (k - Y_LAG) % 2
                if has(g):
                    pe.wait_ge(smat_lo, g + 1)
                    wait(pe, yn_done, g - 1)
                    mm(ps_y[slot][:, :], bs_row[:, :], sw_row[:, :, :], start=True, stop=False)
                    mm(ps_y[slot][:, :], wst_hi[:, :], smat[:, slot, :], start=False, stop=False)
                    mm(ps_y[slot][:, :], wst_lo[:, :], smat[:, slot, :], start=False, stop=True).then_inc(y_done, 1)
                g, slot = s - Z_LAG, (k - Z_LAG) % 2
                if has(g):
                    pe.wait_ge(yn_done, g + 1)
                    wait(pe, zs_done, g)
                    for b in range(GB):
                        j, r = b % BB, b // BB
                        last = mm(ps_z[j * PR:(j + 1) * PR, r * YW:(r + 1) * YW], yn[:, slot, b, 0:PR], yn[:, slot, b, :],
                                  start=True, stop=True)
                    last.then_inc(z_done, 1)
                tile_work(i, k, [(OUTPUTS + o, lambda t, o=o: outputs(t, o)) for o in range(4)]
                          + [(ZVAR, zvar), (LAYER1, lambda t: layer1(t, (0, 1))), (LAYER1 + 1, lambda t: layer1(t, (2, 3))),
                             (LAYER2, layer2), (LAYER3, layer3)])
                if at(s, 2):
                    weights()
                elif at(s, 5):
                    bias1()

            run_steps(pe, step)

        @block.scalar
        def _(act):
            def eps(rows):
                return con[0:rows, CC["eps"][0]:CC["eps"][1]]

            act.wait_ge(set_pe, 5)
            nc.scalar.activation(xsq[:, :], ps_y[0][:, :], ACT.Square).then_inc(set_act, 1)
            act.wait_ge(set_pe, 6)
            nc.scalar.activation(xsq[:, :], ps_a[:, :], ACT.Sqrt, bias=eps(P), scale=1.0 / E).then_inc(set_act, 1)

            def square_z(t):
                act.wait_ge(wl_done, t + 1)
                nc.scalar.activation(zsq[:, :, :], ps_a[:, 0:4 * TB], ACT.Square).then_inc(zsq_done, 1)

            def deviation(t):
                act.wait_ge(zvar_done, t + 1)
                nc.scalar.activation(zstd[:, :], ps_b[:, 0:TB], ACT.Sqrt, bias=eps(P), scale=1.0 / MAXD).then_inc(zstd_done, 1)

            def relu1(t):
                act.wait_ge(l1_done, t + 1)
                for o in range(4):
                    last = nc.scalar.activation(h1[:, o, :], ps_b[:, o * TB:(o + 1) * TB], ACT.Relu, bias=b1f[:, o:o + 1])
                last.then_inc(h1_done, 1)

            def relu2(t):
                act.wait_ge(l2_done, t + 1)
                for o in range(2):
                    last = nc.scalar.activation(h2[:, o, :], ps_b[:, o * TB:(o + 1) * TB], ACT.Relu,
                                                bias=par[:, COLS["b2"][0] + o:COLS["b2"][0] + o + 1])
                last.then_inc(h2_done, 1)

            def result(t):
                act.wait_ge(l3_done, t + 1)
                nc.scalar.activation(y_out[0:1, bass.ds(TB * t, TB)], ps_b[0:1, 2 * TB:3 * TB], ACT.Copy).then_inc(y_ready, 1)

            def step(i, k):
                s = KS * i + k
                if has(s):
                    act.wait_ge(t_done, s + 1)
                    wait(act, quad_done, s - 1)
                    nc.scalar.activation(embt[:, k % 2, :], ps_t[:, 0:2 * R], ACT.Copy).then_inc(embt_done, 1)
                g, slot = s - YN_LAG, (k - YN_LAG) % 2
                if has(g):
                    act.wait_ge(yvar_done, g + 1)
                    nc.scalar.activation(ystd[:, slot, :], yvar[:, slot, :], ACT.Sqrt, bias=eps(P), scale=1.0 / PR).then_inc(ystd_done, 1)
                g, slot = s - S_LAG, (k - S_LAG) % 2
                if has(g):
                    act.wait_ge(s_done, g + 1)
                    wait(act, y_done, g - 1)
                    for h in range(2):
                        nc.scalar.activation(smat[0:D, slot, h * 2 * P:(h + 1) * 2 * P], ps_s[h * D:(h + 1) * D, 0:2 * P],
                                             ACT.Copy).then_inc(smat_hi, 1)
                g, slot = s - G_LAG, (k - G_LAG) % 2
                if has(g):
                    act.wait_ge(evar_done, g + 1)
                    nc.scalar.activation(estd[:, slot, :], evar[:, slot, :], ACT.Sqrt, bias=eps(R), scale=1.0 / E).then_inc(estd_done, 1)
                g, slot = s - Y_LAG, (k - Y_LAG) % 2
                if has(g):
                    act.wait_ge(y_done, g + 1)
                    wait(act, yvar_done, g)
                    nc.scalar.activation(ysq[:, :, :], ps_y[slot][:, :], ACT.Square).then_inc(ysq_done, 1)
                tile_work(i, k, ((ZVAR, square_z), (LAYER3, relu2)))
                g = s - Z_LAG
                if has(g):
                    act.wait_ge(z_done, g + 1)
                    nc.scalar.activation(zs[:, bass.ds(g, 1), :, :], ps_z[:, 0:GT * YW], ACT.Copy).then_inc(zs_done, 1)
                tile_work(i, k, ((ZVAR, deviation), (LAYER1 + 1, relu1), (LAYER3, result)))

            run_steps(act, step)

        @block.vector
        def _(dve):
            v = nc.vector
            links = [0]

            def link(ins):
                links[0] += 1
                ins.then_inc(chain, 1)
                dve.wait_ge(chain, links[0])

            v.memset(gram[:, :], 0.0)
            v.memset(yn[:, :, :, :], 1.0)
            link(v.memset(feat[:, QC, :], 0.0))
            link(v.memset(feat[2 * PR:2 * PR + 1, QC, :], 1.0))
            dve.wait_ge(par_in, 16)
            dve.wait_ge(con_in, 16)
            link(v.reduce_sum(mean[:, 0:1], pv("wsi"), AX_X))
            link(v.tensor_scalar(mean[:, 1:2], mean[:, 0:1], 1.0 / PR, None, ALU.mult))
            link(v.tensor_scalar(wsic[:, :], pv("wsi"), mean[:, 1:2], None, ALU.subtract))
            link(v.tensor_tensor(fold[:, :, :], wsic[0:R, :].unsqueeze(1).to_broadcast([R, BB, PR]),
                                 cv("block", R).unsqueeze(2).to_broadcast([R, BB, PR]), ALU.mult))
            dve.wait_ge(set_pe, 1)
            v.tensor_copy(wsc[:, :], ps_t[:, 0:P]).then_inc(set_dve, 1)
            v.tensor_scalar(wsg[:, :], ps_t[:, 0:P], pv("gs"), None, ALU.mult).then_inc(set_dve, 1)
            v.tensor_copy(mean[:, 15:16], mean[:, 1:2]).then_inc(set_dve, 1)
            dve.wait_ge(wd_in, 16)
            link(v.reduce_sum(mean[:, 2:4], wd[:, :, :], AX_X))
            link(v.tensor_scalar(mean[:, 4:6], mean[:, 2:4], 1.0 / E, None, ALU.mult))
            for c in range(2):
                last = v.tensor_scalar(wd[:, c, :], wd[:, c, :], mean[:, 4 + c:5 + c], None, ALU.subtract)
            last.then_inc(set_dve, 1)
            dve.wait_ge(set_pe, 3)
            for h in range(2):
                v.tensor_copy(gram[h * D:(h + 1) * D, h * D:(h + 1) * D], ps_g[h * D:(h + 1) * D, h * D:(h + 1) * D])
            link(v.tensor_copy(wst[:, :], ps_s[:, 0:P]))
            link(v.tensor_copy(wst_hi[:, :], wst[:, :]))
            v.tensor_tensor(wst_lo[:, :], wst[:, :], wst_hi[:, :].bitcast(F32), ALU.subtract)
            dve.wait_ge(set_pe, 4)
            link(v.tensor_copy(split_f[:, 3, 0:PR], ps_z[0:NSPLIT, 0:PR]))
            for src, parts, width, m0, dst in ((pv("bs", NSPLIT), split_b, E, 0, split_f[:, 2, :]),
                                               (split_f[:, 3, 0:PR], split_s, PR, 3, split_f[:, 2, 0:PR])):
                rest = split_f[:, 0, 0:width]
                link(v.tensor_copy(parts[:, 0, :], src))
                link(v.tensor_tensor(rest, src, parts[:, 0, :], ALU.subtract))
                link(v.tensor_copy(parts[:, 1, :], rest))
                link(v.tensor_tensor(split_f[:, 1, 0:width], rest, parts[:, 1, :], ALU.subtract))
                link(v.tensor_copy(parts[:, 2, :], split_f[:, 1, 0:width]))
                mask = cv("split", NSPLIT)
                link(v.tensor_scalar(dst, parts[:, 0, :], mask[:, m0:m0 + 1], None, ALU.mult))
                link(v.scalar_tensor_tensor(rest, parts[:, 1, :], mask[:, m0 + 1:m0 + 2], dst, ALU.mult, ALU.add))
                link(v.scalar_tensor_tensor(dst, parts[:, 2, :], mask[:, m0 + 2:m0 + 3], rest, ALU.mult, ALU.add))
                if m0 == 0:
                    link(v.tensor_copy(bs_row[:, :], dst))
                else:
                    link(v.tensor_copy(sw_row[:, :, :], dst.unsqueeze(1).to_broadcast([NSPLIT, GB, PR])))
            dve.wait_ge(set_act, 2)
            link(v.reciprocal(xsq[:, :], xsq[:, :]))
            link(v.tensor_tensor(xt[:, :], ps_y[0][:, :], xsq[:, :], ALU.mult))
            v.tensor_scalar(xt[:, :], xt[:, :], pv("gd"), pv("bd"), ALU.mult, ALU.add).then_inc(set_dve, 1)
            dve.wait_ge(set_pe, 7)
            v.tensor_copy(feat[3 * PR:3 * PR + 1, QC, :], ps_b[0:1, :]).then_inc(set_dve, 1)

            def weights1():
                dve.wait_ge(wl_in, 32)
                link(v.reduce_sum(mean[:, 0:QC + 1], wl[:, :, :], AX_X))
                link(v.tensor_scalar(mean[:, 0:QC + 1], mean[:, 0:QC + 1], 1.0 / MAXD, None, ALU.mult))
                for c in range(QC + 1):
                    v.tensor_scalar(wl[:, c, :], wl[:, c, :], mean[:, c:c + 1], None, ALU.subtract)
                mp = cv("mp").unsqueeze(1).to_broadcast([P, QC, PR])
                mq = cv("mq").rearrange("p (c m) -> p c m", c=QC)
                bq = pv("bq")
                v.tensor_scalar(gg[:, :], pv("gq"), pv("gp"), None, ALU.mult)
                link(v.tensor_tensor(sel2[:, :, :], mp, bq.unsqueeze(2).to_broadcast([P, QC, PR]), ALU.mult))
                link(v.tensor_scalar(sel[:, :, 0:PR], mq, pv("bp"), None, ALU.mult))
                v.tensor_scalar(sel[:, :, PR], bq, pv("bp"), float(E), ALU.mult, ALU.mult)
                v.tensor_tensor(sel[:, :, 0:PR], sel[:, :, 0:PR], sel2[:, :, :], ALU.add).then_inc(set_dve, 1)

            def weights2():
                dve.wait_ge(set_pe, 9)
                for c in range(QC):
                    v.tensor_scalar(wl[:, c, :], wl[:, c, :], gg[:, c:c + 1], None, ALU.mult)
                v.tensor_scalar(wl[0:PR, QC, :], wl[0:PR, QC, :], pv("gp", PR), None, ALU.mult)
                v.tensor_scalar(wl[PR:2 * PR, QC, :], ps_a[0:PR, :], pv("gp", PR), None, ALU.mult)
                v.tensor_copy(wl[2 * PR:2 * PR + 1, QC, :], ps_a[PR:PR + 1, :])
                v.tensor_copy(wl[3 * PR:3 * PR + 1, QC, :], ps_b[0:1, :]).then_inc(set_dve, 1)

            def weights3():
                dve.wait_ge(set_pe, 10)
                for c in range(3):
                    v.tensor_scalar(w1[:, c, :], w1[:, c, :], par[:, COLS["gl"][0] + c:COLS["gl"][0] + c + 1], None, ALU.mult)
                v.tensor_tensor(b1f[:, :], ps_a[:, 0:4], pv("b1"), ALU.add).then_inc(set_dve, 1)

            def spread(t, half):
                wait(dve, zs_done, KS * t + 4 * (half + 1))
                src = zs[:, bass.ds(KS * t + 4 * half, 4), :, :].rearrange("p k r c -> p c (k r)")
                dst = feat[:, :, bass.ds(TB * t + TB // 2 * half, TB // 2)].rearrange("p c (m j) -> p c m j", j=BB)
                for u in range(4):
                    n = QC + 1 if u < 2 else QC
                    for j in range(BB):
                        last = v.tensor_copy(dst[u * PR:(u + 1) * PR, 0:n, :, j],
                                             src[j * PR:(j + 1) * PR, u:u + 4 * (n - 1) + 1:4, :])
                last.then_inc(feat_done, 1)

            def normalise(t):
                dve.wait_ge(zstd_done, t + 1)
                v.reciprocal(zrstd[:, :], zstd[:, :]).then_inc(zrstd_done, 1)
                dve.wait_ge(zrstd_done, t + 1)
                v.tensor_tensor(zn[:, :, :], ps_a[:, 0:3 * TB].rearrange("p (o b) -> p o b", b=TB),
                                zrstd[:, :].unsqueeze(1).to_broadcast([P, 3, TB]), ALU.mult).then_inc(zn_done, 1)

            def step(i, k):
                s = KS * i + k
                g, slot, ring = s - G_LAG, (k - G_LAG) % 2, (k - G_LAG) % KS
                rows = emb[:, ring, :].rearrange("p (t d) -> p t d", d=D)
                if has(g):
                    dve.wait_ge(quad_done, g + 1)
                    v.tensor_tensor(prod[:, :, :], ps_g[0:R, 0:GT * D].rearrange("p (t d) -> p t d", d=D), rows, ALU.mult).then_inc(prod_done, 1)
                    dve.wait_ge(prod_done, g + 1)
                    v.reduce_sum(evar[:, slot, :], prod[:, :, :], AX_X).then_inc(evar_done, 1)
                g, slot = s - YN_LAG, (k - YN_LAG) % 2
                if has(g):
                    dve.wait_ge(ystd_done, g + 1)
                    wait(dve, z_done, g - 1)
                    v.reciprocal(yrstd[:, slot, :], ystd[:, slot, :]).then_inc(yrstd_done, 1)
                    v.tensor_copy(yn[:, slot, :, PR], xt[:, bass.ds(GB * g, GB)])
                    dve.wait_ge(yrstd_done, g + 1)
                    v.tensor_tensor(yn[:, slot, :, 0:PR], ps_y[slot][:, :].rearrange("p (g q) -> p g q", q=PR),
                                    yrstd[:, slot, :].unsqueeze(2).to_broadcast([P, GB, PR]), ALU.mult).then_inc(yn_done, 1)
                g, slot = s - S_LAG, (k - S_LAG) % 2
                if has(g):
                    for h in range(2):
                        dve.wait_ge(smat_hi, 2 * g + h + 1)
                        part = smat[:, slot, h * 2 * P:(h + 1) * 2 * P]
                        last = v.tensor_tensor(part[D:2 * D, :], ps_s[h * D:(h + 1) * D, 0:2 * P], part[0:D, :].bitcast(F32), ALU.subtract)
                    last.then_inc(smat_lo, 1)
                g, slot = s - G_LAG, (k - G_LAG) % 2
                if has(g):
                    dve.wait_ge(estd_done, g + 1)
                    v.reciprocal(erstd[:, slot, :], estd[:, slot, :]).then_inc(erstd_done, 1)
                    dve.wait_ge(erstd_done, g + 1)
                    wait(dve, s_done, g - 1)
                    v.tensor_tensor(embs[:, slot, :].rearrange("p (t d) -> p t d", d=D), rows,
                                    erstd[:, slot, :].unsqueeze(2).to_broadcast([R, GT, D]), ALU.mult).then_inc(embs_done, 1)
                tile_work(i, k, ((NORMALISE, normalise),))
                g, slot = s - Y_LAG, (k - Y_LAG) % 2
                if has(g):
                    dve.wait_ge(ysq_done, g + 1)
                    v.reduce_sum(yvar[:, slot, :], ysq[:, :, :], AX_X).then_inc(yvar_done, 1)
                tile_work(i, k, [(SPREAD[half], lambda t, half=half: spread(t, half)) for half in range(2)])
                if at(s, 1):
                    weights1()
                elif at(s, 3):
                    weights2()
                elif at(s, 6):
                    weights3()

            run_steps(dve, step)


def kernel(**inputs):
    import numpy as np
    import concourse.bacc as bacc
    from concourse.bass_utils import run_bass_kernel_spmd as run

    a = {n: np.asarray(x) for n, x in inputs.items()}
    tables = [a[f"tbl_{n}"] for n in range(N)]
    starts = np.concatenate([[0], np.cumsum([t.shape[0] for t in tables])[:-1]]).astype(np.int32)

    def cols(x, n):
        return x.reshape(n, P).T

    par = np.zeros((P, NPAR), np.float32)

    def put(name, x):
        c0, c1 = COLS[name]
        par[:x.shape[0], c0:c1] = x

    gsi, bsi = a["L0_rec_gsi"], a["L0_rec_bsi"]
    put("wsi", np.tile(a["L0_rec_Wsi"].T, (BB, 1)))
    put("gs", cols(a["L0_rec_gs"], 1))
    put("gd", cols(a["L0_rec_gd"], 1))
    put("bd", cols(a["L0_rec_bd"], 1))
    put("gp", np.tile(gsi, 4)[:, None])
    put("bp", np.tile(bsi, 4)[:, None])
    put("gq", np.repeat(gsi.reshape(QC, 4).T, PR, axis=0))
    put("bq", np.repeat(bsi.reshape(QC, 4).T, PR, axis=0))
    put("gl", cols(a["L0_rec_gl"][:DIMS], 3))
    put("bl", cols(a["L0_rec_bl"][:DIMS], 3))
    put("b1", cols(a["b_top1"], 4))
    put("b2", cols(a["b_top2"], 2))
    put("w3", cols(a["W_top3"][:, 0], 2))
    put("bs", np.tile(a["L0_rec_bs"], (NSPLIT, 1)))

    con = np.zeros((P, NCON), np.float32)
    rows = np.arange(P)

    def const(name, x):
        c0, c1 = CC[name]
        con[:x.shape[0], c0:c1] = x

    const("ident", np.eye(P))
    const("centre", np.eye(P) - 1.0 / E)
    const("ones", np.ones((P, P)))
    const("eps", np.full((P, 1), EPS))
    const("block", rows[:R, None] // N == np.arange(BB))
    const("mp", rows[:, None] % PR == np.arange(PR))
    const("mq", (rows[:, None, None] // PR + 4 * np.arange(QC)[:, None] == np.arange(PR)).reshape(P, -1))
    const("split", np.concatenate([rows[:NSPLIT, None] // 3 == np.arange(3), rows[:NSPLIT, None] % 3 == np.arange(3)], 1))

    wl = np.zeros((4, PR, QC, MAXD), np.float32)
    wlt = a["L0_rec_Wl"].T
    for p in range(PR):
        for q in range(p):
            wl[q % 4, p, q // 4] = wlt[(p + 1) * p // 2 + q + 1]
    wx = wlt[[(p + 1) * p // 2 for p in range(PR)]]

    w1 = a["W_top1"]
    arrays = {
        "table": np.concatenate(tables, axis=0),
        "ids": a["ids"].reshape(B // GB, 2, 2, R).transpose(3, 0, 2, 1).reshape(R, B // BB),
        "base": np.tile(starts, BB)[:, None],
        "par": par,
        "con": con,
        "ws": np.concatenate([a["L0_rec_Ws"]] * 2, axis=1),
        "wd": a["L0_rec_Wd"].T.reshape(2, P, E).transpose(1, 0, 2),
        "dense": a["r_dense_t"].T.reshape(2, P, B).transpose(1, 0, 2),
        "wl": wl.reshape(P, QC, MAXD),
        "wx": wx,
        "w1": np.concatenate([w1[:DIMS], w1[MAXD:]]).reshape(5, P, H1).transpose(1, 0, 2),
        "w2": a["W_top2"].reshape(4, P, H2).transpose(1, 0, 2),
    }
    arrays = {n: np.ascontiguousarray(x) for n, x in arrays.items()}

    nc = bacc.Bacc("TRN2", target_bir_lowering=False, num_devices=1)
    args = [nc.dram_tensor(f"in_{n}", x.shape, mybir.dt.from_np(x.dtype), kind="ExternalInput").ap() for n, x in arrays.items()]
    out = nc.dram_tensor("out", (1, B), F32, kind="ExternalOutput").ap()
    dlrm_program(nc, *args, out)
    r = run(nc, [{f"in_{n}": x for n, x in arrays.items()}], core_ids=[0])
    return r.results[0]["out"].reshape(B, 1)
```

```python
from contextlib import ExitStack

import concourse.bass as bass
from concourse import mybir

F32 = mybir.dt.float32
F32R = mybir.dt.float32r
BF16 = mybir.dt.bfloat16
I32 = mybir.dt.int32
ALU = mybir.AluOpType
ACT = mybir.ActivationFunctionType
AX_X = mybir.AxisListType.X

P = 128
B = 512
N = 26
D = 64
E = 128
PR = 32
MAXD, DIMS = 512, 384
H1, H2 = 512, 256
EPS = 1e-5

BB = P // PR
R = BB * N
GT = 4
GB = BB * GT
KS = 8
TB = GB * KS
TILES = B // TB
G_LAG, S_LAG, Y_LAG, YN_LAG, Z_LAG = 1, 2, 3, 4, 5
OUTPUTS, NORMALISE, LAYER1, LAYER2, LAYER3 = 14, 18, 18, 22, 23
OUTPUT_PARTS = (0, 1, 10, 19, 27)
LAYER1_PARTS = (0, 2, 8, 14, 20)
ACT_SPREAD = ((8, 0, (0, 1)), (9, 0, (2, 3)), (12, 1, (0, 1)), (13, 1, (2,)))
DVE_SPREAD = ((13, 1, (3,)),)
SPLIT = (11, 14)
LAST_ACT_SPREAD = ((8, 0, (0, 1)), (9, 0, (2, 3)), (12, 1, (0, 1)))
LAST_DVE_SPREAD = ((12, 1, (2, 3)),)
LAST_SPLIT = (11, 13)
LAST_OUTPUT_PARTS = (0, 9, 27)
LAST_OUTPUTS = 13
BACK = LAYER3 // KS
STEPS = (TILES - 1) * KS + LAST_OUTPUTS + 1
QC = 8
YW = PR + 2
NSPLIT = 9

COLS = {}


def _cols():
    at = 0
    for name, width in [("wsi", PR), ("gs", 1), ("gd", 1), ("bd", 1), ("gp", 1), ("bp", 1), ("gq", QC + 1),
                        ("bq", QC), ("gl", 3), ("bl", 3), ("b1", 4), ("b2", 2), ("w3", 2), ("bs", E)]:
        COLS[name] = (at, at + width)
        at += width
    return at


NPAR = _cols()

CC = {}


def _ccols():
    at = 0
    for name, width in [("ident", P), ("centre", P), ("ones", P), ("eps", 1), ("block", BB), ("mp", PR),
                        ("mq", QC * PR), ("split", 6)]:
        CC[name] = (at, at + width)
        at += width
    return at


NCON = _ccols()


def dlrm_program(nc, table, ids, par_d, con_d, ws_d, wd_d, dense_d, wl_d, wx_d, w1_d, w2_d, out):
    with ExitStack() as ctx:
        def sb(name, shape, dt=F32):
            return ctx.enter_context(nc.sbuf_tensor(name, shape, dt))

        def sem(name):
            return ctx.enter_context(nc.semaphore(name))

        par = sb("par", [P, NPAR])
        con = sb("con", [P, NCON])
        idx_all = sb("idx_all", [R, B // BB + 1], I32)
        idx = sb("idx", [R, KS, GT], I32)
        pace = sb("pace", [R, 1], I32)
        ws2 = sb("ws2", [P, P])
        wsc = sb("wsc", [P, P])
        wsg = sb("wsg", [P, P])
        wst_hi = sb("wst_hi", [P, P], F32R)
        wst_lo = sb("wst_lo", [P, P], F32R)
        gram = sb("gram", [P, P])
        wsic = sb("wsic", [P, PR])
        fold = sb("fold", [R, BB, PR])
        wd = sb("wd", [P, 2, E])
        dense = sb("dense", [P, 2, B])
        wl_raw = sb("wl_raw", [P, QC + 1, MAXD])
        wl_part = sb("wl_part", [P, 2, MAXD])
        wl_last = sb("wl_last", [P, MAXD])
        wl_hi = sb("wl_hi", [P, QC + 1, MAXD], F32R)
        wl_lo = sb("wl_lo", [P, QC + 1, MAXD], F32R)
        w1 = sb("w1", [P, 5, H1])
        w2 = sb("w2", [P, 4, H2])
        bs_row = sb("bs_row", [NSPLIT, E], BF16)
        sw_row = sb("sw_row", [NSPLIT, GB, PR], BF16)
        split_in = sb("split_in", [NSPLIT, E + PR])
        split_rest = sb("split_rest", [NSPLIT, 2, E + PR])
        split_part = sb("split_part", [NSPLIT, 3, E + PR], BF16)
        split_sel = sb("split_sel", [NSPLIT, 2, E + PR])
        mean = sb("mean", [P, 8])
        wl_mean = sb("wl_mean", [P, QC + 1])
        wl_bias = sb("wl_bias", [P, QC + 1])
        wl_pass = sb("wl_pass", [P, MAXD])
        fold_mean = sb("fold_mean", [P, 4])
        gg = sb("gg", [P, QC + 1])
        sel = sb("sel", [P, QC, PR + 1])
        sel2 = sb("sel2", [P, QC, PR])
        xt = sb("xt", [P, B])
        xrow = sb("xrow", [P, 4, E])
        xsq = sb("xsq", [P, E])
        xvar = sb("xvar", [P, 4])
        xstd = sb("xstd", [P, 4])
        xrstd = sb("xrstd", [P, 4])
        emb = sb("emb", [R, KS, GT * D])
        embt = sb("embt", [P, 2, 2 * R])
        prod = sb("prod", [R, GT, D])
        evar = sb("evar", [R, 2, GT])
        estd = sb("estd", [R, 2, GT])
        erstd = sb("erstd", [R, 2, GT])
        embs = sb("embs", [R, 2, GT * D])
        smat = sb("smat", [P, 2, GB * PR], F32R)
        ysq = sb("ysq", [P, GB, PR])
        yvar = sb("yvar", [P, 2, GB])
        ystd = sb("ystd", [P, 2, GB])
        yrstd = sb("yrstd", [P, 2, GB])
        yn = sb("yn", [P, 2, GB, YW])
        zs = sb("zs", [P, B // GB, GT, YW])
        feat = sb("feat", [P, QC + 1, B])
        feat_hi = sb("feat_hi", [P, QC + 1, TB], F32R)
        feat_lo = sb("feat_lo", [P, QC + 1, TB], F32R)
        zsq = sb("zsq", [P, MAXD])
        zvar = sb("zvar", [P, 1])
        zstd = sb("zstd", [P, 1])
        zrstd = sb("zrstd", [P, 1])
        zrow = sb("zrow", [P, 3, P])
        zn = sb("zn", [P, 3, TB])
        h1 = sb("h1", [P, 4, TB])
        h2 = sb("h2", [P, 2, TB])
        y_out = sb("y_out", [1, B])

        def pb(name):
            return ctx.enter_context(nc.psum_tensor(name, [P, 512], F32))

        ps_t, ps_g, ps_s, ps_z, ps_a, ps_b = (pb(f"ps_{n}") for n in "tgszab")
        ps_y = [pb(f"ps_y{n}") for n in range(2)]
        tail_zt = (ps_t, ps_g, ps_s)
        tail_l1 = (ps_y[0], ps_y[1], ps_z, ps_a)
        tail_l2 = (ps_t, ps_g)

        def pv(name, rows=P):
            a, b = COLS[name]
            return par[0:rows, a:b]

        def cv(name, rows=P):
            a, b = CC[name]
            return con[0:rows, a:b]

        ids_in, par_in, con_in, ws_in = sem("ids_in"), sem("par_in"), sem("con_in"), sem("ws_in")
        dense_in, wd_in, wx_in, w1_in, w2_in = sem("dense_in"), sem("wd_in"), sem("wx_in"), sem("w1_in"), sem("w2_in")
        wl_in = [sem(f"wl_in{n}") for n in range(4)]
        emb_in = [sem(f"emb_in{k}") for k in range(KS)]
        out_done = sem("out_done")
        idx_done = sem("idx_done")
        cleared = sem("cleared")
        chain = sem("chain")
        ones_set, table_warm = sem("ones_set"), sem("table_warm")
        wsc_mm, gram_mm, wst_mm, sw_mm = sem("wsc_mm"), sem("gram_mm"), sem("wst_mm"), sem("sw_mm")
        fold_done = sem("fold_done")
        wsic_done, wsc_done, wsg_done = sem("wsic_done"), sem("wsc_done"), sem("wsg_done")
        wd_done, group_weights, rows_done = sem("wd_done"), sem("group_weights"), sem("rows_done")
        x_mm, xvar_done, xstd_done, xrow_done = sem("x_mm"), sem("xvar_done"), sem("xstd_done"), sem("xrow_done")
        xt_mm, xt_done, xsum_mm, xsum_done = sem("xt_mm"), sem("xt_done"), sem("xsum_mm"), sem("xsum_done")
        sel_done, fold_mm, wsum_done, wl_bias_done = sem("sel_done"), sem("fold_mm"), sem("wsum_done"), sem("wl_bias_done")
        fold_mean_done, wl_split = sem("fold_mean_done"), sem("wl_split")
        feat_hi_done, feat_lo_done = sem("feat_hi_done"), sem("feat_lo_done")
        wl_scaled, wl_folded = sem("wl_scaled"), sem("wl_folded")
        t_done, embt_done, quad_done, evar_done = sem("t_done"), sem("embt_done"), sem("quad_done"), sem("evar_done")
        estd_done, embs_done, s_done = sem("estd_done"), sem("embs_done"), sem("s_done")
        smat_hi, smat_lo = sem("smat_hi"), sem("smat_lo")
        y_done, ysq_done, yvar_done, ystd_done = sem("y_done"), sem("ysq_done"), sem("yvar_done"), sem("ystd_done")
        prod_done, erstd_done, yrstd_done, zrstd_done = sem("prod_done"), sem("erstd_done"), sem("yrstd_done"), sem("zrstd_done")
        yn_done, z_done, zs_done = sem("yn_done"), sem("z_done"), sem("zs_done")
        feat_act, feat_dve = sem("feat_act"), sem("feat_dve")
        wl_done, zsq_done, zrow_done, zt_mm = sem("wl_done"), sem("zsq_done"), sem("zrow_done"), sem("zt_mm")
        zstd_done, zn_done, l1_done, h1_done = sem("zstd_done"), sem("zn_done"), sem("l1_done"), sem("h1_done")
        h1_dve, h2_dve = sem("h1_dve"), sem("h2_dve")
        l2_done, h2_done, l3_done, y_ready = sem("l2_done"), sem("h2_done"), sem("l3_done"), sem("y_ready")

        block = ctx.enter_context(nc.Block())

        def wait(eng, s, value):
            if not isinstance(value, int) or value > 0:
                eng.wait_ge(s, value)

        def has(s):
            return not isinstance(s, int) or 0 <= s < TILES * KS

        def at(s, n):
            return isinstance(s, int) and s == n

        def tile_work(i, k, works, last_works=()):
            for offset, work in works:
                t = i - offset // KS
                if offset % KS == k and (not isinstance(t, int) or 0 <= t < TILES - 1):
                    work(t)
            for offset, work in last_works:
                if isinstance(i, int) and KS * (TILES - 1) + offset == KS * i + k:
                    work(TILES - 1)

        def spread(eng, copy, t, half, blocks, done):
            wait(eng, zs_done, KS * t + 4 * (half + 1))
            src = zs[:, bass.ds(KS * t + 4 * half, 4), :, :].rearrange("p k r c -> p c (k r)")
            dst = feat[:, :, bass.ds(TB * t + TB // 2 * half, TB // 2)].rearrange("p c (m j) -> p c m j", j=BB)
            for u in blocks:
                n = QC + 1 if u < 2 else QC
                for j in range(BB):
                    last = copy(dst[u * PR:(u + 1) * PR, 0:n, :, j], src[j * PR:(j + 1) * PR, u:u + 4 * (n - 1) + 1:4, :])
            last.then_inc(done, 1)

        def in_steps(work):
            return lambda t: None if isinstance(t, int) and t == TILES - 2 else work(t)

        def run_steps(eng, step):
            for i in range(BACK):
                for k in range(KS):
                    step(i, k)
            with eng.Fori(BACK, TILES) as i:
                for k in range(KS):
                    step(i, k)
            for s in range(TILES * KS, STEPS):
                step(s // KS, s % KS)

        @block.sync
        def _(sp):
            sp.dma_start(idx_all[:, :], ids).then_inc(ids_in, 16)
            sp.dma_start(ws2[:, :], ws_d).then_inc(ws_in, 16)
            sp.dma_start(con[:, :], con_d).then_inc(con_in, 16)
            sp.dma_start(par[:, :], par_d).then_inc(par_in, 16)
            sp.dma_start(wd[:, :, :], wd_d).then_inc(wd_in, 16)
            for n in range(4):
                if n > 1:
                    sp.wait_ge(emb_in[n - 2], 16 * GT)
                if n == 2:
                    sp.dma_start(dense[:, :, :], dense_d).then_inc(dense_in, 16)
                sp.dma_start(wl_raw[:, 2 * n:2 * n + 2, :], wl_d[:, 2 * n:2 * n + 2, :]).then_inc(wl_in[n], 16)
            sp.wait_ge(cleared, 2)
            sp.dma_start(wl_raw[0:PR, QC, :], wx_d).then_inc(wx_in, 16)
            for n in range(2):
                sp.wait_ge(emb_in[2 + n], 16 * GT)
                cs = slice(3 * n, 3 + 2 * n)
                sp.dma_start(w1[:, cs, :], w1_d[:, cs, :]).then_inc(w1_in, 16)
            sp.wait_ge(emb_in[4], 16 * GT)
            sp.dma_start(w2[:, :, :], w2_d).then_inc(w2_in, 16)
            sp.wait_ge(y_ready, TILES)
            sp.dma_start(out, y_out[0:1, :]).then_inc(out_done, 16)
            sp.wait_ge(out_done, 16)

        @block.gpsimd
        def _(pool):
            nc.gpsimd.memset(gram[:, :], 0.0).then_inc(cleared, 1)
            nc.gpsimd.memset(wl_raw[:, QC, :], 0.0).then_inc(cleared, 1)
            nc.gpsimd.memset(feat[:, QC, :], 0.0).then_inc(cleared, 1)
            nc.gpsimd.memset(wl_last[:, :], 0.0).then_inc(cleared, 1)
            pool.wait_ge(ids_in, 16)
            base = idx_all[:, B // BB:B // BB + 1]

            def gather_tile(i):
                for k in range(KS):
                    if k % 4 == 0:
                        wait(pool, embs_done, KS * i - KS + k + 4)
                        nc.gpsimd.tensor_tensor(idx[:, k:k + 4, :].rearrange("p k t -> p (k t)"),
                                                idx_all[:, bass.ds(KS * GT * i + k * GT, 4 * GT)],
                                                base.to_broadcast([R, 4 * GT]), ALU.add).then_inc(idx_done, 1)
                        pool.wait_ge(idx_done, 2 * i + k // 4 + 1)
                        nc.gpsimd.tensor_tensor(pace[:, :], base, base, ALU.add)
                    for t in range(GT):
                        nc.gpsimd.indirect_dma_start(
                            emb[:, k, t * D:(t + 1) * D], None, table,
                            bass.IndirectOffsetOnAxis(ap=idx[:, k, t:t + 1], axis=0)
                        ).then_inc(emb_in[k], 16)

            gather_tile(0)
            with pool.Fori(1, TILES) as i:
                gather_tile(i)

        @block.tensor
        def _(pe):
            mm = nc.tensor.matmul
            pe.wait_ge(con_in, 16)
            pe.wait_ge(ws_in, 16)
            mm(ps_t[:, 0:P], cv("centre"), ws2[:, :], start=True, stop=True).then_inc(wsc_mm, 1)
            pe.wait_ge(wsc_done, 1)
            mm(ps_g[:, 0:P], wsc[:, :], wsc[:, :], start=True, stop=True).then_inc(gram_mm, 1)
            pe.wait_ge(wsg_done, 1)
            nc.tensor.transpose(ps_s[:, 0:P], wsg[:, :], cv("ident")).then_inc(wst_mm, 1)
            pe.wait_ge(wsic_done, 1)
            mm(ps_z[0:NSPLIT, 0:PR], con[0:N, CC["ones"][0]:CC["ones"][0] + NSPLIT], wsic[0:N, :],
               start=True, stop=True).then_inc(sw_mm, 1)

            def x_project():
                pe.wait_ge(wd_done, 1)
                pe.wait_ge(dense_in, 16)
                for m in range(4):
                    for c in range(2):
                        last = mm(ps_a[:, m * E:(m + 1) * E], dense[:, c, m * P:(m + 1) * P], wd[:, c, :],
                                  start=c == 0, stop=c == 1)
                last.then_inc(x_mm, 1)

            def x_transpose():
                pe.wait_ge(xrow_done, 1)
                for m in range(4):
                    last = nc.tensor.transpose(ps_b[:, m * P:(m + 1) * P], xrow[:, m, :], cv("ident"))
                last.then_inc(xt_mm, 1)

            def x_sum():
                pe.wait_ge(xt_done, 1)
                mm(ps_b[0:1, :], con[:, CC["ones"][0]:CC["ones"][0] + 1], xt[:, :], start=True, stop=True).then_inc(xsum_mm, 1)

            def fold_bsi(chunks):
                if chunks[0] == 0:
                    pe.wait_ge(sel_done, 1)
                pe.wait_ge(wl_in[chunks[0] // 2], 16)
                for c in chunks:
                    last = mm(ps_a[0:PR + 1, :], sel[:, c, :], wl_raw[:, c, :], start=c == 0, stop=c == QC - 1)
                if c == QC - 1:
                    last.then_inc(fold_mm, 1)
                    pe.wait_ge(wx_in, 16)
                    mm(ps_a[2 * PR:2 * PR + 1, :], par[0:PR, COLS["bp"][0]:COLS["bp"][1]], wl_raw[0:PR, QC, :],
                       start=True, stop=True).then_inc(fold_mm, 1)

            first_steps = {1: x_project, 2: x_transpose, 3: lambda: fold_bsi((0, 1)), 8: x_sum,
                           **{3 + n: (lambda n=n: fold_bsi((2 * n, 2 * n + 1))) for n in range(1, 4)}}

            products = [(w, feat_hi, c) for c in range(QC + 1) for w in (wl_hi, wl_lo)]
            low_from = len(products)
            products += [(wl_hi, feat_lo, c) for c in range(QC + 1)]

            def outputs(t, part, parts=OUTPUT_PARTS):
                if part == 0:
                    pe.wait_ge(feat_hi_done, 2 * t + 2)
                    pe.wait_ge(wl_folded, 1)
                    wait(pe, zn_done, t)
                for n in range(parts[part], parts[part + 1]):
                    w, f, c = products[n]
                    if n < low_from:
                        pe.wait_ge(wl_split, c + 1)
                    if n == low_from:
                        pe.wait_ge(feat_lo_done, 2 * t + 2)
                    last = mm(ps_a[:, :], f[:, c, :], w[:, c, :], start=n == 0, stop=n == len(products) - 1)
                if part == len(parts) - 2:
                    last.then_inc(wl_done, 1)

            def z_transpose(t):
                pe.wait_ge(zrow_done, t + 1)
                for c in range(3):
                    last = nc.tensor.transpose(ps_a[:, c * TB:(c + 1) * TB], zrow[:, c, :], cv("ident"))
                last.then_inc(zt_mm, 1)

            layer1_products = [(o, c) for o in range(4) for c in (3, 4, 0, 1, 2)]

            def layer1(t, part):
                if part == 0:
                    pe.wait_ge(w1_in, 32)
                    wait(pe, y_ready, t)
                for n in range(LAYER1_PARTS[part], LAYER1_PARTS[part + 1]):
                    o, c = layer1_products[n]
                    if n == 2:
                        pe.wait_ge(zn_done, t + 1)
                    rhs = zn[:, c, :] if c < 3 else dense[:, c - 3, bass.ds(TB * t, TB)]
                    last = mm(ps_b[:, o * TB:(o + 1) * TB], w1[:, c, o * P:(o + 1) * P], rhs, start=c == 3, stop=c == 2)
                if part == 3:
                    last.then_inc(l1_done, 1)

            def layer2(t):
                pe.wait_ge(h1_done, t + 1)
                pe.wait_ge(w2_in, 16)
                for o in range(2):
                    for c in range(4):
                        last = mm(ps_b[:, o * TB:(o + 1) * TB], w2[:, c, o * P:(o + 1) * P], h1[:, c, :],
                                  start=c == 0, stop=c == 3)
                last.then_inc(l2_done, 1)

            def layer3(t):
                pe.wait_ge(h2_done, t + 1)
                for c in range(2):
                    last = mm(ps_b[0:1, 2 * TB:3 * TB], par[:, COLS["w3"][0] + c:COLS["w3"][0] + c + 1], h2[:, c, :],
                              start=c == 0, stop=c == 1)
                last.then_inc(l3_done, 1)

            def step(i, k):
                s = KS * i + k
                if has(s):
                    wait(pe, embt_done, s)
                    pe.wait_ge(emb_in[k], 16 * GT * i + 16 * GT)
                    for h in range(2):
                        last = nc.tensor.transpose(ps_t[:, h * R:(h + 1) * R], emb[:, k, h * P:(h + 1) * P],
                                                   con[0:R, CC["ident"][0]:CC["ident"][0] + R])
                    last.then_inc(t_done, 1)
                g, slot = s - G_LAG, (k - G_LAG) % 2
                if has(g):
                    if at(g, 0):
                        pe.wait_ge(group_weights, 1)
                    pe.wait_ge(embt_done, g + 1)
                    wait(pe, prod_done, g)
                    for h in range(2):
                        last = mm(ps_g[0:R, h * P:(h + 1) * P], embt[:, slot, h * R:(h + 1) * R], gram[:, :],
                                  start=True, stop=True)
                    last.then_inc(quad_done, 1)
                g, slot = s - S_LAG, (k - S_LAG) % 2
                if has(g):
                    if at(g, 0):
                        pe.wait_ge(fold_done, 1)
                    pe.wait_ge(embs_done, g + 1)
                    wait(pe, smat_lo, g)
                    for h in range(2):
                        last = mm(ps_s[:, h * P:(h + 1) * P], embs[:, slot, h * P:(h + 1) * P],
                                  fold[:, :, :], start=True, stop=True)
                    last.then_inc(s_done, 1)
                g, slot = s - Y_LAG, (k - Y_LAG) % 2
                if has(g):
                    if at(g, 0):
                        pe.wait_ge(rows_done, 1)
                    pe.wait_ge(smat_lo, g + 1)
                    wait(pe, yn_done, g - 1)
                    mm(ps_y[slot][:, :], bs_row[:, :], sw_row[:, :, :], start=True, stop=False)
                    mm(ps_y[slot][:, :], wst_hi[:, :], smat[:, slot, :], start=False, stop=False)
                    mm(ps_y[slot][:, :], wst_lo[:, :], smat[:, slot, :], start=False, stop=True).then_inc(y_done, 1)
                g, slot = s - Z_LAG, (k - Z_LAG) % 2
                if has(g):
                    pe.wait_ge(yn_done, g + 1)
                    wait(pe, zs_done, g)
                    for b in range(GB):
                        j, r = b % BB, b // BB
                        last = mm(ps_z[j * PR:(j + 1) * PR, r * YW:(r + 1) * YW], yn[:, slot, b, 0:PR], yn[:, slot, b, :],
                                  start=True, stop=True)
                    last.then_inc(z_done, 1)
                tile_work(i, k, [(LAYER2, in_steps(layer2))] + [(OUTPUTS + n, lambda t, n=n: outputs(t, n)) for n in range(4)]
                          + [(LAYER1, lambda t: layer1(t, 0)), (NORMALISE, z_transpose),
                             (LAYER1 + 1, lambda t: layer1(t, 1)), (LAYER1 + 2, lambda t: layer1(t, 2)),
                             (LAYER1 + 3, lambda t: layer1(t, 3)), (LAYER3, in_steps(layer3))],
                          [(LAST_OUTPUTS, lambda t: outputs(t, 0, LAST_OUTPUT_PARTS))])
                if isinstance(s, int) and s in first_steps:
                    first_steps[s]()

            run_steps(pe, step)

            def last_tile():
                t = TILES - 1

                def dense_part(o):
                    for c in (3, 4):
                        mm(tail_l1[o][:, 0:TB], w1[:, c, o * P:(o + 1) * P], dense[:, c - 3, TB * t:TB * (t + 1)],
                           start=c == 3, stop=False)

                outputs(t, 1, LAST_OUTPUT_PARTS)
                layer2(t - 1)
                for o in range(3):
                    dense_part(o)
                for c in range(3):
                    pe.wait_ge(zrow_done, t + c + 1)
                    nc.tensor.transpose(tail_zt[c][:, 0:TB], zrow[:, c, :], cv("ident")).then_inc(zt_mm, 1)
                dense_part(3)
                for c in range(3):
                    pe.wait_ge(zn_done, t + c + 1)
                    for o in range(4):
                        last = mm(tail_l1[o][:, 0:TB], w1[:, c, o * P:(o + 1) * P], zn[:, c, :], start=False, stop=c == 2)
                        if c == 2:
                            last.then_inc(l1_done, 1)
                layer3(t - 1)
                for c in range(4):
                    if c % 2:
                        pe.wait_ge(h1_dve, (c + 1) // 2)
                    else:
                        pe.wait_ge(h1_done, t + c // 2 + 1)
                    for o in range(2):
                        last = mm(tail_l2[o][:, 0:TB], w2[:, c, o * P:(o + 1) * P], h1[:, c, :], start=c == 0, stop=c == 3)
                        if c == 3:
                            last.then_inc(l2_done, 1)
                pe.wait_ge(h2_done, t + 1)
                pe.wait_ge(h2_dve, 1)
                for c in range(2):
                    last = mm(ps_s[0:1, 0:TB], par[:, COLS["w3"][0] + c:COLS["w3"][0] + c + 1], h2[:, c, :],
                              start=c == 0, stop=c == 1)
                last.then_inc(l3_done, 1)

            last_tile()

        @block.scalar
        def _(act):
            def eps(rows):
                return con[0:rows, CC["eps"][0]:CC["eps"][1]]

            act.wait_ge(ones_set, 1)
            nc.scalar.activation(xstd[:, 0:1], yn[:, 0, 0, PR + 1:PR + 2], ACT.Sqrt).then_inc(table_warm, 1)

            def x_variance():
                act.wait_ge(x_mm, 1)
                for m in range(4):
                    nc.scalar.activation(xsq[:, :], ps_a[:, m * E:(m + 1) * E], ACT.Square,
                                         accum_out=xvar[:, m:m + 1]).then_inc(xvar_done, 1)
                    act.wait_ge(xvar_done, m + 1)
                act.wait_ge(table_warm, 1)
                nc.scalar.activation(xstd[:, :], xvar[:, :], ACT.Sqrt, bias=eps(P), scale=1.0 / E).then_inc(xstd_done, 1)

            def x_affine():
                act.wait_ge(xt_mm, 1)
                nc.scalar.activation(xt[:, :], ps_b[:, :], ACT.Identity, bias=pv("bd"), scale=pv("gd")).then_inc(xt_done, 1)

            def wl_sums(chunks):
                for c in chunks:
                    if c == QC:
                        act.wait_ge(wx_in, 16)
                    else:
                        act.wait_ge(wl_in[c // 2], 16)
                    wait(act, wsum_done, c)
                    nc.scalar.activation(wl_pass[:, :], wl_raw[:, c, :], ACT.Copy, accum_out=wl_mean[:, c:c + 1]).then_inc(wsum_done, 1)

            def folded_weights():
                act.wait_ge(fold_mean_done, 1)
                act.wait_ge(cleared, 4)
                nc.scalar.activation(wl_last[PR:2 * PR, :], ps_a[0:PR, :], ACT.Identity, bias=fold_mean[0:PR, 2:3], scale=pv("gp", PR))
                nc.scalar.activation(wl_last[2 * PR:2 * PR + 1, :], ps_a[PR:PR + 1, :], ACT.Identity, bias=fold_mean[PR:PR + 1, 2:3])
                nc.scalar.activation(wl_last[3 * PR:3 * PR + 1, :], ps_a[2 * PR:2 * PR + 1, :], ACT.Identity,
                                     bias=fold_mean[2 * PR:2 * PR + 1, 2:3]).then_inc(wl_folded, 1)

            def wl_scale(chunks):
                act.wait_ge(wl_bias_done, 1)
                act.wait_ge(cleared, 4)
                for c in chunks:
                    rows, part = (P, wl_part[:, c % 2, :]) if c < QC else (PR, wl_last[0:PR, :])
                    wait(act, wl_split, c - 1 if c < QC else 0)
                    for dst in (part, wl_hi[0:rows, c, :]) if c < QC else (part,):
                        nc.scalar.activation(dst, wl_raw[0:rows, c, :], ACT.Identity,
                                             bias=wl_bias[0:rows, c:c + 1], scale=gg[0:rows, c:c + 1]).then_inc(wl_scaled, 1)
                    if c == QC:
                        act.wait_ge(wl_scaled, 2 * QC + 1)
                        act.wait_ge(wl_folded, 1)
                        nc.scalar.activation(wl_hi[:, c, :], wl_last[:, :], ACT.Copy).then_inc(wl_scaled, 1)

            wl_sums((0, 1, 2, 3))
            first_steps = {0: lambda: wl_sums((4, 5)), 1: lambda: (x_variance(), wl_sums((6,))),
                           2: lambda: (x_affine(), wl_sums((7, 8))), 10: folded_weights,
                           **{s: (lambda c=c: wl_scale((c,))) for c, s in enumerate((3, 4, 5, 6, 7, 11, 13, 14, 15))}}

            def copy(dst, src):
                return nc.scalar.activation(dst, src, ACT.Copy)

            def wait_features(t, half):
                last = isinstance(t, int) and t == TILES - 1
                act.wait_ge(feat_act, len(ACT_SPREAD) * t + (len(LAST_ACT_SPREAD) if half and last else 2 * (half + 1)))
                if half:
                    act.wait_ge(feat_dve, len(DVE_SPREAD) * (t + 1))
                wait(act, wl_done, t)
                act.wait_ge(xsum_done, 1)

            def feat_high(t, half):
                rows = bass.ds(TB * t + TB // 2 * half, TB // 2)
                nc.scalar.activation(feat_hi[:, :, half * TB // 2:(half + 1) * TB // 2], feat[:, :, rows], ACT.Copy).then_inc(feat_hi_done, 1)

            def deviation(t):
                act.wait_ge(wl_done, t + 1)
                nc.scalar.activation(zsq[:, :], ps_a[:, :], ACT.Square, accum_out=zvar[:, :]).then_inc(zsq_done, 1)
                act.wait_ge(zsq_done, t + 1)
                nc.scalar.activation(zstd[:, :], zvar[:, :], ACT.Sqrt, bias=eps(P), scale=1.0 / MAXD).then_inc(zstd_done, 1)

            def normalise(t):
                act.wait_ge(zrstd_done, t + 1)
                nc.scalar.activation(zrow[:, :, :], ps_a[:, 0:DIMS], ACT.Copy, scale=zrstd[:, 0:1]).then_inc(zrow_done, 1)

            def affine_z(c, src):
                gl, bl = COLS["gl"][0] + c, COLS["bl"][0] + c
                return nc.scalar.activation(zn[:, c, :], src, ACT.Identity, bias=par[:, bl:bl + 1], scale=par[:, gl:gl + 1])

            def take_transposed(t):
                act.wait_ge(zt_mm, t + 1)
                for c in range(3):
                    last = affine_z(c, ps_a[:, c * TB:(c + 1) * TB])
                last.then_inc(zn_done, 1)

            def relu1(t):
                act.wait_ge(l1_done, t + 1)
                for o in range(4):
                    last = nc.scalar.activation(h1[:, o, :], ps_b[:, o * TB:(o + 1) * TB], ACT.Relu, bias=par[:, COLS["b1"][0] + o:COLS["b1"][0] + o + 1])
                last.then_inc(h1_done, 1)

            def relu2(t):
                act.wait_ge(l2_done, t + 1)
                for o in range(2):
                    last = nc.scalar.activation(h2[:, o, :], ps_b[:, o * TB:(o + 1) * TB], ACT.Relu,
                                                bias=par[:, COLS["b2"][0] + o:COLS["b2"][0] + o + 1])
                last.then_inc(h2_done, 1)

            def result(t):
                act.wait_ge(l3_done, t + 1)
                nc.scalar.activation(y_out[0:1, bass.ds(TB * t, TB)], ps_b[0:1, 2 * TB:3 * TB], ACT.Copy).then_inc(y_ready, 1)

            def step(i, k):
                s = KS * i + k
                if has(s):
                    act.wait_ge(t_done, s + 1)
                    wait(act, quad_done, s - 1)
                    nc.scalar.activation(embt[:, k % 2, :], ps_t[:, 0:2 * R], ACT.Copy).then_inc(embt_done, 1)
                tile_work(i, k, *([(offset, lambda t, half=half: wait_features(t, half)) for half, offset in enumerate(steps)]
                                  for steps in (SPLIT, LAST_SPLIT)))
                tile_work(i, k, ((NORMALISE, deviation),))
                g, slot = s - YN_LAG, (k - YN_LAG) % 2
                if has(g):
                    act.wait_ge(yvar_done, g + 1)
                    nc.scalar.activation(ystd[:, slot, :], yvar[:, slot, :], ACT.Sqrt, bias=eps(P), scale=1.0 / PR).then_inc(ystd_done, 1)
                tile_work(i, k, *([(offset, lambda t, half=half: feat_high(t, half)) for half, offset in enumerate(steps)]
                                  for steps in (SPLIT, LAST_SPLIT)))
                g, slot = s - S_LAG, (k - S_LAG) % 2
                if has(g):
                    act.wait_ge(s_done, g + 1)
                    wait(act, y_done, g - 1)
                    for h in range(2):
                        nc.scalar.activation(smat[0:D, slot, h * 2 * P:(h + 1) * 2 * P], ps_s[h * D:(h + 1) * D, 0:2 * P],
                                             ACT.Copy).then_inc(smat_hi, 1)
                tile_work(i, k, ((NORMALISE, normalise),))
                g, slot = s - G_LAG, (k - G_LAG) % 2
                if has(g):
                    act.wait_ge(evar_done, g + 1)
                    nc.scalar.activation(estd[:, slot, :], evar[:, slot, :], ACT.Sqrt, bias=eps(R), scale=1.0 / E).then_inc(estd_done, 1)
                g, slot = s - Y_LAG, (k - Y_LAG) % 2
                if has(g):
                    act.wait_ge(y_done, g + 1)
                    wait(act, yvar_done, g)
                    nc.scalar.activation(ysq[:, :, :], ps_y[slot][:, :], ACT.Square).then_inc(ysq_done, 1)
                tile_work(i, k, ((LAYER3, in_steps(relu2)),))
                g = s - Z_LAG
                if has(g):
                    act.wait_ge(z_done, g + 1)
                    nc.scalar.activation(zs[:, bass.ds(g, 1), :, :], ps_z[:, 0:GT * YW], ACT.Copy).then_inc(zs_done, 1)
                tile_work(i, k, ((NORMALISE, take_transposed), (LAYER1 + 3, relu1), (LAYER3, in_steps(result))))
                tile_work(i, k, *([(offset, lambda t, half=half, us=us: spread(act, copy, t, half, us, feat_act))
                                   for offset, half, us in steps] for steps in (ACT_SPREAD, LAST_ACT_SPREAD)))
                if isinstance(s, int) and s in first_steps:
                    first_steps[s]()

            run_steps(act, step)

            def last_tile():
                t = TILES - 1
                deviation(t)
                for c in range(3):
                    act.wait_ge(zt_mm, t + c + 1)
                    affine_z(c, tail_zt[c][:, 0:TB]).then_inc(zn_done, 1)
                relu2(t - 1)
                for o in (0, 2):
                    act.wait_ge(l1_done, t + o + 1)
                    nc.scalar.activation(h1[:, o, :], tail_l1[o][:, 0:TB], ACT.Relu, bias=par[:, COLS["b1"][0] + o:COLS["b1"][0] + o + 1]).then_inc(h1_done, 1)
                result(t - 1)
                act.wait_ge(l2_done, t + 1)
                nc.scalar.activation(h2[:, 0, :], tail_l2[0][:, 0:TB], ACT.Relu,
                                     bias=par[:, COLS["b2"][0]:COLS["b2"][0] + 1]).then_inc(h2_done, 1)
                act.wait_ge(l3_done, t + 1)
                nc.scalar.activation(y_out[0:1, TB * t:TB * (t + 1)], ps_s[0:1, 0:TB], ACT.Copy).then_inc(y_ready, 1)

            last_tile()

        @block.vector
        def _(dve):
            v = nc.vector
            links = [0]

            def link(ins):
                links[0] += 1
                ins.then_inc(chain, 1)
                dve.wait_ge(chain, links[0])

            v.memset(yn[:, :, :, PR + 1], 1.0).then_inc(ones_set, 1)
            dve.wait_ge(par_in, 16)
            dve.wait_ge(wsc_mm, 1)
            v.tensor_copy(wsc[:, :], ps_t[:, 0:P]).then_inc(wsc_done, 1)
            v.tensor_scalar(wsg[:, :], ps_t[:, 0:P], pv("gs"), None, ALU.mult).then_inc(wsg_done, 1)
            link(v.reduce_sum(mean[:, 0:1], pv("wsi"), AX_X))
            link(v.tensor_scalar(mean[:, 1:2], mean[:, 0:1], 1.0 / PR, None, ALU.mult))
            v.tensor_scalar(wsic[:, :], pv("wsi"), mean[:, 1:2], None, ALU.subtract).then_inc(wsic_done, 1)
            dve.wait_ge(gram_mm, 1)
            dve.wait_ge(cleared, 1)
            for h in range(2):
                last = v.tensor_copy(gram[h * D:(h + 1) * D, h * D:(h + 1) * D], ps_g[h * D:(h + 1) * D, h * D:(h + 1) * D])
            last.then_inc(group_weights, 1)
            dve.wait_ge(wsic_done, 1)
            dve.wait_ge(con_in, 16)
            v.tensor_tensor(fold[:, :, :], wsic[0:R, :].unsqueeze(1).to_broadcast([R, BB, PR]),
                            cv("block", R).unsqueeze(2).to_broadcast([R, BB, PR]), ALU.mult).then_inc(fold_done, 1)
            dve.wait_ge(wd_in, 16)
            link(v.reduce_sum(mean[:, 2:4], wd[:, :, :], AX_X))
            link(v.tensor_scalar(mean[:, 4:6], mean[:, 2:4], 1.0 / E, None, ALU.mult))
            for c in range(2):
                last = v.tensor_scalar(wd[:, c, :], wd[:, c, :], mean[:, 4 + c:5 + c], None, ALU.subtract)
            last.then_inc(wd_done, 1)
            dve.wait_ge(wst_mm, 1)
            link(v.tensor_copy(wst_hi[:, :], ps_s[:, 0:P]))
            v.tensor_tensor(wst_lo[:, :], ps_s[:, 0:P], wst_hi[:, :].bitcast(F32), ALU.subtract)
            v.tensor_copy(split_in[:, 0:E], pv("bs", NSPLIT))
            dve.wait_ge(sw_mm, 1)
            link(v.tensor_copy(split_in[:, E:E + PR], ps_z[0:NSPLIT, 0:PR]))
            link(v.tensor_copy(split_part[:, 0, :], split_in[:, :]))
            link(v.tensor_tensor(split_rest[:, 0, :], split_in[:, :], split_part[:, 0, :], ALU.subtract))
            link(v.tensor_copy(split_part[:, 1, :], split_rest[:, 0, :]))
            link(v.tensor_tensor(split_rest[:, 1, :], split_rest[:, 0, :], split_part[:, 1, :], ALU.subtract))
            link(v.tensor_copy(split_part[:, 2, :], split_rest[:, 1, :]))
            mask = cv("split", NSPLIT)
            sides = ((slice(0, E), 0), (slice(E, E + PR), 3))
            for cols_, m in sides:
                last = v.tensor_scalar(split_sel[:, 0, cols_], split_part[:, 0, cols_], mask[:, m:m + 1], None, ALU.mult)
            link(last)
            for n in range(2):
                for cols_, m in sides:
                    last = v.scalar_tensor_tensor(split_sel[:, 1 - n, cols_], split_part[:, 1 + n, cols_],
                                                  mask[:, m + 1 + n:m + 2 + n], split_sel[:, n, cols_], ALU.mult, ALU.add)
                link(last)
            v.tensor_copy(bs_row[:, :], split_sel[:, 0, 0:E])
            v.tensor_copy(sw_row[:, :, :], split_sel[:, 0, E:E + PR].unsqueeze(1).to_broadcast([NSPLIT, GB, PR])).then_inc(rows_done, 1)

            def x_normalise():
                dve.wait_ge(xstd_done, 1)
                link(v.reciprocal(xrstd[:, :], xstd[:, :]))
                v.tensor_tensor(xrow[:, :, :], ps_a[:, :].rearrange("p (m e) -> p m e", e=E),
                                xrstd[:, :].unsqueeze(2).to_broadcast([P, 4, E]), ALU.mult).then_inc(xrow_done, 1)

            def select():
                mp = cv("mp").unsqueeze(1).to_broadcast([P, QC, PR])
                mq = cv("mq").rearrange("p (c m) -> p c m", c=QC)
                bq = pv("bq")
                v.tensor_scalar(gg[:, :], pv("gq"), pv("gp"), None, ALU.mult)
                v.tensor_scalar(sel[:, :, PR], bq, pv("bp"), float(E), ALU.mult, ALU.mult)
                v.tensor_tensor(sel2[:, :, :], mp, bq.unsqueeze(2).to_broadcast([P, QC, PR]), ALU.mult)
                link(v.tensor_scalar(sel[:, :, 0:PR], mq, pv("bp"), None, ALU.mult))
                v.tensor_tensor(sel[:, :, 0:PR], sel[:, :, 0:PR], sel2[:, :, :], ALU.add).then_inc(sel_done, 1)

            def sum_feature():
                dve.wait_ge(xsum_mm, 1)
                dve.wait_ge(cleared, 3)
                v.memset(feat[2 * PR:2 * PR + 1, QC, :], 1.0)
                v.tensor_copy(feat[3 * PR:3 * PR + 1, QC, :], ps_b[0:1, :]).then_inc(xsum_done, 1)

            def wl_biases():
                dve.wait_ge(wsum_done, QC + 1)
                link(v.tensor_tensor(wl_bias[:, :], wl_mean[:, :], gg[:, :], ALU.mult))
                v.tensor_scalar(wl_bias[:, :], wl_bias[:, :], -1.0 / MAXD, None, ALU.mult).then_inc(wl_bias_done, 1)

            def fold_means():
                dve.wait_ge(fold_mm, 2)
                v.reduce_sum(fold_mean[0:PR + 1, 0:1], ps_a[0:PR + 1, :], AX_X)
                link(v.reduce_sum(fold_mean[2 * PR:2 * PR + 1, 0:1], ps_a[2 * PR:2 * PR + 1, :], AX_X))
                v.tensor_scalar(fold_mean[0:PR, 2:3], fold_mean[0:PR, 0:1], pv("gp", PR), -1.0 / MAXD, ALU.mult, ALU.mult)
                v.tensor_scalar(fold_mean[PR:PR + 1, 2:3], fold_mean[PR:PR + 1, 0:1], -1.0 / MAXD, None, ALU.mult)
                v.tensor_scalar(fold_mean[2 * PR:2 * PR + 1, 2:3], fold_mean[2 * PR:2 * PR + 1, 0:1], -1.0 / MAXD, None, ALU.mult).then_inc(fold_mean_done, 1)

            def wl_low(c):
                dve.wait_ge(wl_scaled, 2 * c + 2)
                part = wl_part[:, c % 2, :] if c < QC else wl_last[:, :]
                v.tensor_tensor(wl_lo[:, c, :], part, wl_hi[:, c, :].bitcast(F32), ALU.subtract).then_inc(wl_split, 1)

            first_steps = {1: x_normalise, 2: lambda: (select(), wl_biases()), 4: lambda: wl_low(0), 10: sum_feature,
                           5: lambda: wl_low(1), 6: lambda: wl_low(2), 7: fold_means, 8: lambda: wl_low(3), 9: lambda: wl_low(4),
                           12: lambda: wl_low(5), 14: lambda: wl_low(6), 15: lambda: (wl_low(7), wl_low(8))}

            def feat_low(t, half):
                dve.wait_ge(feat_hi_done, 2 * t + half + 1)
                part = slice(half * TB // 2, (half + 1) * TB // 2)
                rows = bass.ds(TB * t + TB // 2 * half, TB // 2)
                v.tensor_tensor(feat_lo[:, :, part], feat[:, :, rows], feat_hi[:, :, part].bitcast(F32),
                                ALU.subtract).then_inc(feat_lo_done, 1)

            def invert_deviation(t):
                dve.wait_ge(zstd_done, t + 1)
                v.reciprocal(zrstd[:, :], zstd[:, :]).then_inc(zrstd_done, 1)

            def step(i, k):
                s = KS * i + k
                g, slot, ring = s - G_LAG, (k - G_LAG) % 2, (k - G_LAG) % KS
                rows = emb[:, ring, :].rearrange("p (t d) -> p t d", d=D)
                if has(g):
                    dve.wait_ge(quad_done, g + 1)
                    v.tensor_tensor(prod[:, :, :], ps_g[0:R, 0:GT * D].rearrange("p (t d) -> p t d", d=D), rows, ALU.mult).then_inc(prod_done, 1)
                tile_work(i, k, ((NORMALISE, invert_deviation),))
                if has(g):
                    dve.wait_ge(prod_done, g + 1)
                    v.reduce_sum(evar[:, slot, :], prod[:, :, :], AX_X).then_inc(evar_done, 1)
                g, slot = s - YN_LAG, (k - YN_LAG) % 2
                if has(g):
                    dve.wait_ge(ystd_done, g + 1)
                    wait(dve, z_done, g - 1)
                    v.reciprocal(yrstd[:, slot, :], ystd[:, slot, :]).then_inc(yrstd_done, 1)
                    if at(g, 0):
                        dve.wait_ge(xt_done, 1)
                    v.tensor_copy(yn[:, slot, :, PR], xt[:, bass.ds(GB * g, GB)])
                    dve.wait_ge(yrstd_done, g + 1)
                    v.tensor_tensor(yn[:, slot, :, 0:PR], ps_y[slot][:, :].rearrange("p (g q) -> p g q", q=PR),
                                    yrstd[:, slot, :].unsqueeze(2).to_broadcast([P, GB, PR]), ALU.mult).then_inc(yn_done, 1)
                g, slot = s - S_LAG, (k - S_LAG) % 2
                if has(g):
                    for h in range(2):
                        dve.wait_ge(smat_hi, 2 * g + h + 1)
                        part = smat[:, slot, h * 2 * P:(h + 1) * 2 * P]
                        last = v.tensor_tensor(part[D:2 * D, :], ps_s[h * D:(h + 1) * D, 0:2 * P], part[0:D, :].bitcast(F32), ALU.subtract)
                    last.then_inc(smat_lo, 1)
                tile_work(i, k, *([(offset, lambda t, half=half: feat_low(t, half)) for half, offset in enumerate(steps)]
                                  for steps in (SPLIT, LAST_SPLIT)))
                g, slot = s - G_LAG, (k - G_LAG) % 2
                if has(g):
                    dve.wait_ge(estd_done, g + 1)
                    v.reciprocal(erstd[:, slot, :], estd[:, slot, :]).then_inc(erstd_done, 1)
                    dve.wait_ge(erstd_done, g + 1)
                    wait(dve, s_done, g - 1)
                    v.tensor_tensor(embs[:, slot, :].rearrange("p (t d) -> p t d", d=D), rows,
                                    erstd[:, slot, :].unsqueeze(2).to_broadcast([R, GT, D]), ALU.mult).then_inc(embs_done, 1)
                g, slot = s - Y_LAG, (k - Y_LAG) % 2
                if has(g):
                    dve.wait_ge(ysq_done, g + 1)
                    v.reduce_sum(yvar[:, slot, :], ysq[:, :, :], AX_X).then_inc(yvar_done, 1)
                tile_work(i, k, *([(offset, lambda t, half=half, us=us: spread(dve, v.tensor_copy, t, half, us, feat_dve))
                                   for offset, half, us in steps] for steps in (DVE_SPREAD, LAST_DVE_SPREAD)))
                if isinstance(s, int) and s in first_steps:
                    first_steps[s]()

            run_steps(dve, step)

            def last_tile():
                t = TILES - 1
                invert_deviation(t)
                dve.wait_ge(zrstd_done, t + 1)
                for c in range(3):
                    v.tensor_scalar(zrow[:, c, :], ps_a[:, c * P:(c + 1) * P], zrstd[:, :], None, ALU.mult).then_inc(zrow_done, 1)
                dve.wait_ge(l2_done, t)
                for o in (1, 3):
                    dve.wait_ge(l1_done, t + o + 1)
                    v.tensor_scalar(h1[:, o, :], tail_l1[o][:, 0:TB], par[:, COLS["b1"][0] + o:COLS["b1"][0] + o + 1], 0.0, ALU.add, ALU.max).then_inc(h1_dve, 1)
                dve.wait_ge(l3_done, t)
                dve.wait_ge(l2_done, t + 2)
                v.tensor_scalar(h2[:, 1, :], tail_l2[1][:, 0:TB], par[:, COLS["b2"][0] + 1:COLS["b2"][0] + 2], 0.0,
                                ALU.add, ALU.max).then_inc(h2_dve, 1)

            last_tile()


def kernel(**inputs):
    import numpy as np
    import concourse.bacc as bacc
    from concourse.bass_utils import run_bass_kernel_spmd as run

    a = {n: np.asarray(x) for n, x in inputs.items()}
    tables = [a[f"tbl_{n}"] for n in range(N)]
    starts = np.concatenate([[0], np.cumsum([t.shape[0] for t in tables])[:-1]]).astype(np.int32)

    def cols(x, n):
        return x.reshape(n, P).T

    par = np.zeros((P, NPAR), np.float32)

    def put(name, x):
        c0, c1 = COLS[name]
        par[:x.shape[0], c0:c1] = x

    gsi, bsi = a["L0_rec_gsi"], a["L0_rec_bsi"]
    put("wsi", np.tile(a["L0_rec_Wsi"].T, (BB, 1)))
    put("gs", cols(a["L0_rec_gs"], 1))
    put("gd", cols(a["L0_rec_gd"], 1))
    put("bd", cols(a["L0_rec_bd"], 1))
    put("gp", np.tile(gsi, 4)[:, None])
    put("bp", np.tile(bsi, 4)[:, None])
    put("gq", np.concatenate([np.repeat(gsi.reshape(QC, 4).T, PR, axis=0), np.ones((P, 1), np.float32)], axis=1))
    put("bq", np.repeat(bsi.reshape(QC, 4).T, PR, axis=0))
    put("gl", cols(a["L0_rec_gl"][:DIMS], 3))
    put("bl", cols(a["L0_rec_bl"][:DIMS], 3))
    put("b1", cols(a["b_top1"], 4))
    put("b2", cols(a["b_top2"], 2))
    put("w3", cols(a["W_top3"][:, 0], 2))
    put("bs", np.tile(a["L0_rec_bs"], (NSPLIT, 1)))

    con = np.zeros((P, NCON), np.float32)
    rows = np.arange(P)

    def const(name, x):
        c0, c1 = CC[name]
        con[:x.shape[0], c0:c1] = x

    const("ident", np.eye(P))
    const("centre", np.eye(P) - 1.0 / E)
    const("ones", np.ones((P, P)))
    const("eps", np.full((P, 1), EPS))
    const("block", rows[:R, None] // N == np.arange(BB))
    const("mp", rows[:, None] % PR == np.arange(PR))
    const("mq", (rows[:, None, None] // PR + 4 * np.arange(QC)[:, None] == np.arange(PR)).reshape(P, -1))
    const("split", np.concatenate([rows[:NSPLIT, None] // 3 == np.arange(3), rows[:NSPLIT, None] % 3 == np.arange(3)], 1))

    wl = np.zeros((4, PR, QC, MAXD), np.float32)
    wlt = a["L0_rec_Wl"].T
    for p in range(PR):
        for q in range(p):
            wl[q % 4, p, q // 4] = wlt[(p + 1) * p // 2 + q + 1]
    wx = wlt[[(p + 1) * p // 2 for p in range(PR)]]

    w1 = a["W_top1"]
    arrays = {
        "table": np.concatenate(tables, axis=0),
        "ids": np.concatenate([a["ids"].reshape(B // GB, 2, 2, R).transpose(3, 0, 2, 1).reshape(R, B // BB),
                               np.tile(starts, BB)[:, None]], axis=1),
        "par": par,
        "con": con,
        "ws": np.concatenate([a["L0_rec_Ws"]] * 2, axis=1),
        "wd": a["L0_rec_Wd"].T.reshape(2, P, E).transpose(1, 0, 2),
        "dense": a["r_dense_t"].T.reshape(2, P, B).transpose(1, 0, 2),
        "wl": wl.reshape(P, QC, MAXD),
        "wx": wx,
        "w1": np.concatenate([w1[:DIMS], w1[MAXD:]]).reshape(5, P, H1).transpose(1, 0, 2),
        "w2": a["W_top2"].reshape(4, P, H2).transpose(1, 0, 2),
    }
    arrays = {n: np.ascontiguousarray(x) for n, x in arrays.items()}

    nc = bacc.Bacc("TRN2", target_bir_lowering=False, num_devices=1)
    args = [nc.dram_tensor(f"in_{n}", x.shape, mybir.dt.from_np(x.dtype), kind="ExternalInput").ap() for n, x in arrays.items()]
    out = nc.dram_tensor("out", (1, B), F32, kind="ExternalOutput").ap()
    dlrm_program(nc, *args, out)
    r = run(nc, [{f"in_{n}": x for n, x in arrays.items()}], core_ids=[0])
    return r.results[0]["out"].reshape(B, 1)
```
